# Optimizing a Trainium2 kernel written in Bass

```python
import numpy as np
import jax
import jax.numpy as jnp

def _softmax(x, axis=-1):
    return jax.nn.softmax(x, axis=axis)

def _gelu(x):
    return jax.nn.gelu(x, approximate=True)

def _silu(x):
    return jax.nn.silu(x)

def _sigmoid(x):
    return jax.nn.sigmoid(x)

def _layernorm(x, axis=-1, eps=1e-05):
    m = jnp.mean(x, axis=axis, keepdims=True)
    v = jnp.var(x, axis=axis, keepdims=True)
    return (x - m) / jnp.sqrt(v + eps)

def _scatter_add(tgt, idx, src, axis=0):
    return tgt.at[idx].add(src)

def _segment_sum(src, seg, n):
    return jax.ops.segment_sum(src, seg, n)
kernel_name = 'mk_seq_preln_d1_jaxref_r8_ad7ada'

def setup_inputs(seed: int=0):
    np.random.seed(seed)
    _w = jnp.asarray

    def _L0_attn_setup():
        import jax, jax.numpy as jnp
        import numpy as np
        HIDDEN = 512
        NH = 32
        NKV = 8
        HD = 128
        GS = 128
        BASE = 10000.0
        B, S = (2, 256)

        def _dequant(codes, scales):
            w = codes.astype(jnp.float32) - 8.0
            return w * jnp.repeat(scales, GS, axis=0)

        def _rope(x):
            s, d = (x.shape[2], x.shape[3])
            pos = jnp.arange(s, dtype=jnp.float32)
            inv_freq = 1.0 / BASE ** (jnp.arange(0, d, 2, dtype=jnp.float32) / d)
            f = pos[:, None] * inv_freq[None, :]
            cos = jnp.cos(f)[None, None]
            sin = jnp.sin(f)[None, None]
            xe = x[..., ::2]
            xo = x[..., 1::2]
            re = xe * cos - xo * sin
            ro = xo * cos + xe * sin
            return jnp.stack([re, ro], axis=-1).reshape(x.shape)
        key = jax.random.key(seed)
        ks = jax.random.split(key, 9)

        def codes(k, i, o):
            return jax.random.randint(k, (i, o), 0, 16, dtype=jnp.int32)

        def scales(k, i, o):
            return jax.random.uniform(k, (i // GS, o), dtype=jnp.float32) * 0.02
        return {'hidden_states': jax.random.normal(ks[0], (B, S, HIDDEN), jnp.float32), 'q_codes': codes(ks[1], HIDDEN, NH * HD), 'q_scales': scales(ks[2], HIDDEN, NH * HD), 'k_codes': codes(ks[3], HIDDEN, NKV * HD), 'k_scales': scales(ks[4], HIDDEN, NKV * HD), 'v_codes': codes(ks[5], HIDDEN, NKV * HD), 'v_scales': scales(ks[6], HIDDEN, NKV * HD), 'o_codes': codes(ks[7], NH * HD, HIDDEN), 'o_scales': scales(ks[8], NH * HD, HIDDEN)}
    _L0_attn_in = _L0_attn_setup()

    def _L0_ffn_setup():
        import jax, jax.numpy as jnp
        import numpy as np
        HD, M = (512, 1792)
        key = jax.random.key(seed)
        k_x, k_g, k_u, k_d = jax.random.split(key, 4)
        scale = 1.0 / np.sqrt(HD)
        x = jax.random.normal(k_x, (4, 256, HD), dtype=jnp.float16)
        W_gate = jax.random.normal(k_g, (M, HD), dtype=jnp.float16) * jnp.float16(scale)
        W_up = jax.random.normal(k_u, (M, HD), dtype=jnp.float16) * jnp.float16(scale)
        W_down = jax.random.normal(k_d, (HD, M), dtype=jnp.float16) * jnp.float16(1.0 / np.sqrt(M))
        return {'x': x, 'W_gate': W_gate, 'W_up': W_up, 'W_down': W_down}
    _L0_ffn_in = _L0_ffn_setup()
    _d = {'L0_attn_hidden_states': _L0_attn_in['hidden_states'], 'L0_attn_q_codes': _L0_attn_in['q_codes'], 'L0_attn_q_scales': _L0_attn_in['q_scales'], 'L0_attn_k_codes': _L0_attn_in['k_codes'], 'L0_attn_k_scales': _L0_attn_in['k_scales'], 'L0_attn_v_codes': _L0_attn_in['v_codes'], 'L0_attn_v_scales': _L0_attn_in['v_scales'], 'L0_attn_o_codes': _L0_attn_in['o_codes'], 'L0_attn_o_scales': _L0_attn_in['o_scales'], 'L0_ffn_W_gate': _L0_ffn_in['W_gate'], 'L0_ffn_W_up': _L0_ffn_in['W_up'], 'L0_ffn_W_down': _L0_ffn_in['W_down']}
    _x0 = _d['L0_attn_hidden_states']
    _d['L0_attn_hidden_states'] = jax.random.normal(jax.random.fold_in(jax.random.key(seed), 1), (4, 256, 512), dtype=_x0.dtype)
    del _x0
    return _d

def reference(L0_attn_hidden_states, L0_attn_q_codes, L0_attn_q_scales, L0_attn_k_codes, L0_attn_k_scales, L0_attn_v_codes, L0_attn_v_scales, L0_attn_o_codes, L0_attn_o_scales, L0_ffn_W_gate, L0_ffn_W_up, L0_ffn_W_down):

    def _L0_attn_ref(hidden_states, q_codes, q_scales, k_codes, k_scales, v_codes, v_scales, o_codes, o_scales):
        import jax, jax.numpy as jnp
        import numpy as np
        HIDDEN = 512
        NH = 32
        NKV = 8
        HD = 128
        GS = 128
        BASE = 10000.0
        B, S = (2, 256)

        def _dequant(codes, scales):
            w = codes.astype(jnp.float32) - 8.0
            return w * jnp.repeat(scales, GS, axis=0)

        def _rope(x):
            s, d = (x.shape[2], x.shape[3])
            pos = jnp.arange(s, dtype=jnp.float32)
            inv_freq = 1.0 / BASE ** (jnp.arange(0, d, 2, dtype=jnp.float32) / d)
            f = pos[:, None] * inv_freq[None, :]
            cos = jnp.cos(f)[None, None]
            sin = jnp.sin(f)[None, None]
            xe = x[..., ::2]
            xo = x[..., 1::2]
            re = xe * cos - xo * sin
            ro = xo * cos + xe * sin
            return jnp.stack([re, ro], axis=-1).reshape(x.shape)
        b, s, _ = hidden_states.shape
        q = hidden_states @ _dequant(q_codes, q_scales)
        k = hidden_states @ _dequant(k_codes, k_scales)
        v = hidden_states @ _dequant(v_codes, v_scales)
        q = q.reshape(b, s, NH, HD).transpose(0, 2, 1, 3)
        k = k.reshape(b, s, NKV, HD).transpose(0, 2, 1, 3)
        v = v.reshape(b, s, NKV, HD).transpose(0, 2, 1, 3)
        q = _rope(q)
        k = _rope(k)
        rf = NH // NKV
        k = jnp.repeat(k, rf, axis=1)
        v = jnp.repeat(v, rf, axis=1)
        scale = HD ** (-0.5)
        causal = jnp.tril(jnp.ones((s, s), dtype=bool))
        mask = jnp.where(causal, 0.0, -jnp.inf).astype(q.dtype)
        scores = jnp.einsum('bhqd,bhkd->bhqk', q, k) * scale + mask[None, None]
        attn = jax.nn.softmax(scores, axis=-1)
        out = jnp.einsum('bhqk,bhkd->bhqd', attn, v)
        out = out.transpose(0, 2, 1, 3).reshape(b, s, NH * HD)
        return out @ _dequant(o_codes, o_scales)

    def _L0_ffn_ref(x, W_gate, W_up, W_down):
        import jax, jax.numpy as jnp
        import numpy as np
        HD, M = (512, 1792)
        gate = jnp.einsum('bsh,mh->bsm', x, W_gate)
        up = jnp.einsum('bsh,mh->bsm', x, W_up)
        h = jax.nn.silu(gate) * up
        out = jnp.einsum('bsm,hm->bsh', h, W_down)
        return out
    x = L0_attn_hidden_states
    x = x + _L0_attn_ref(_layernorm(x, axis=-1), L0_attn_q_codes, L0_attn_q_scales, L0_attn_k_codes, L0_attn_k_scales, L0_attn_v_codes, L0_attn_v_scales, L0_attn_o_codes, L0_attn_o_scales)
    x = x + _L0_ffn_ref(_layernorm(x, axis=-1), L0_ffn_W_gate, L0_ffn_W_up, L0_ffn_W_down)
    return x

_drawn_inputs = setup_inputs


def setup_inputs(seed=0):
    import zlib

    import numpy as np

    out = dict(_drawn_inputs(seed))
    spreads = {}
    factors = {}
    for name, (base, spread) in spreads.items():
        noise = np.random.default_rng([zlib.crc32(name.encode()), seed]).standard_normal(out[name].shape)
        drawn = base * np.exp(spread * noise) if base else spread * noise
        out[name] = jnp.asarray(drawn.astype(out[name].dtype))
    for name, factor in factors.items():
        out[name] = (out[name] * factor).astype(out[name].dtype)
    return out
```

```python
from contextlib import ExitStack

import concourse.bass as bass
from concourse import mybir

F32 = mybir.dt.float32
F32R = mybir.dt.float32r
F16 = mybir.dt.float16
I32 = mybir.dt.int32
ALU = mybir.AluOpType
ACT = mybir.ActivationFunctionType

P = 128
BATCH, SEQ, HID = 4, 256, 512
TOK = BATCH * SEQ
TT = TOK // P
KT = HID // P
NH, NKV = 32, 8
HPG = NH // NKV
FFN = 1792
MT = FFN // P
MH = MT // 2
HALF = 512
NHALF = TOK // HALF
STEPS = 2 * BATCH
UNITS = 1 + HPG
TRI = P + SEQ
SCALE = P ** -0.5
EPS = 1e-5
OFFSET = -8.0
MASKED = -3.0e38


def f(ap):
    return ap.bitcast(F32)


def layer_kernel(nc, x, qc, qs, kc, ks, vc, vs, oc, os_, wg, wu, wd, rope_cos, rope_sin, causal, eye, out):
    v_hi_d = nc.dram_tensor("v_hi_scratch", (NKV, TT, P, P), F32, kind="Internal").ap()
    v_lo_d = nc.dram_tensor("v_lo_scratch", (NKV, TT, P, P), F32, kind="Internal").ap()

    with ExitStack() as whole:
        def sem(name):
            return whole.enter_context(nc.semaphore(name))

        def sb(name, shape, dt, ctx=whole):
            return ctx.enter_context(nc.sbuf_tensor(name, shape, dt))

        def bank(name):
            return whole.enter_context(nc.psum_tensor(name, [P, HALF], F32))

        ps_unit = [bank(f"ps_unit{i}") for i in range(2)]
        ps_s = [bank(f"ps_s{i}") for i in range(2)]
        ps_t = [bank(f"ps_t{i}") for i in range(2)]
        ps_pv = bank("ps_pv")
        ps_o = bank("ps_o")

        acc = sb("acc", [P, TT, HID], F32)
        xn_hi = sb("xn_hi", [P, KT, TOK], F32R)
        xn_lo = sb("xn_lo", [P, KT, TOK], F32R)
        rot = [sb(f"rot{i}", [P, HALF], F32) for i in range(2)]
        rot_a = sb("rot_a", [P, HALF], F32)
        ident = sb("ident", [P, P], F32)
        bn = sb("bn", [P, TT, 6], F32)
        mv = sb("mv", [P, TT, 2], F32)
        ln = sb("ln", [P, 6, TT], F32)
        maxs = sb("maxs", [P, 2, 4], F32)
        nmax = sb("nmax", [P, 2, 4], F32)
        rsum = sb("rsum", [P, 2, 4], F32)
        rinv = sb("rinv", [P, 2, 4], F32)

        d_x = [sem(f"d_x{t}") for t in range(TT)]
        d_const = sem("d_const")
        d_vw = [sem(f"d_vw{c}") for c in range(2)]
        d_vout = [sem(f"d_vout{i}") for i in range(4)]
        d_vin = [sem(f"d_vin{b}") for b in range(BATCH)]
        d_kw, d_qw, d_oc, d_os = sem("d_kw"), sem("d_qw"), sem("d_oc"), sem("d_os")
        d_gu, d_wd = sem("d_gu"), sem("d_wd")
        d_out = sem("d_out")
        ln_bn, ln_mv, ln_var, ln_sqrt, ln_chain = sem("ln_bn"), sem("ln_mv"), sem("ln_var"), sem("ln_sqrt"), sem("ln_chain")
        ln_xn, ln_t, ln_hi, ln_lo = sem("ln_xn"), sem("ln_t"), sem("ln_hi"), sem("ln_lo")
        vw_prod, vw_hi, vw_lo = sem("vw_prod"), sem("vw_hi"), sem("vw_lo")
        v_mm, v_hi, v_lo = sem("v_mm"), sem("v_hi"), sem("v_lo")
        w_prod, w_hi, w_lo = sem("w_prod"), sem("w_hi"), sem("w_lo")
        o_prod, o_hi, o_lo_p, o_lo_v = sem("o_prod"), sem("o_hi"), sem("o_lo_p"), sem("o_lo_v")
        u_mm, u_swap, u_cos, u_sin, u_rot, u_hi, u_lo = (sem(n) for n in ("u_mm", "u_swap", "u_cos", "u_sin", "u_rot", "u_hi", "u_lo"))
        s_mm, s_max, s_neg, s_exp, s_inv, s_nrm = (sem(n) for n in ("s_mm", "s_max", "s_neg", "s_exp", "s_inv", "s_nrm"))
        s_seen = sem("s_seen")
        t_mm, t_hi, t_lo = sem("t_mm"), sem("t_hi"), sem("t_lo")
        pv_mm, pv_hi, pv_lo = sem("pv_mm"), sem("pv_hi"), sem("pv_lo")
        o_mm, o_add = sem("o_mm"), sem("o_add")
        f_wcast, f_gu, f_sg, f_h, f_hi, f_lo, f_dcast, f_dn, f_add = (
            sem(n) for n in ("f_wcast", "f_gu", "f_sg", "f_h", "f_hi", "f_lo", "f_dcast", "f_dn", "f_add"))

        def after_head(g, s, j):
            return 2 * STEPS * g + (2 * s + j + 1)

        def after_tile(g, s, j, i):
            return 4 * STEPS * g + (4 * s + 2 * j + i + 1)

        def after_step(g, s):
            return STEPS * g + (s + 1)

        def after_unit(g, half, w):
            return 2 * UNITS * g + (UNITS * half + w + 1)

        def after_weight(g, w):
            return UNITS * g + (w + 1)

        def after_out(g, b, i):
            return TT * g + (2 * b + i + 1)

        def units_of(s, last):
            if s >= STEPS:
                return []
            if s < 4:
                return ([(0, 1, 0)] if s == 0 else []) + [(0, 1, 1 + s)]
            return [] if last else ([(1, 0, 0)] if s == 4 else []) + [(1, 0, 1 + s - 4)]

        def weights_of(s, last):
            return [] if last else {1: [0], 3: [1], 4: [2], 5: [3], 6: [4]}.get(s, [])

        def groups(eng, body):
            body(0, True, False)
            with eng.Fori(1, NKV - 1) as g:
                body(g, False, False)
            body(NKV - 1, False, True)

        def earlier(g):
            return not (isinstance(g, int) and g == 0)

        q_codes = sb("q_codes", [P, HPG, KT, P], I32)
        q_scale = sb("q_scale", [P, HPG, KT, P], F32)
        o_codes = sb("o_codes", [P, HPG, HID], I32)
        o_scale = sb("o_scale", [P, HPG, HID], F32)
        gate_16 = [b.bitcast(F16)[:, 0:MH * KT * P].rearrange("p (m k c) -> p m k c", m=MH, k=KT)
                   for b in (q_codes[:].rearrange("p h k d -> p (h k d)"), q_scale[:].rearrange("p h k d -> p (h k d)"))]
        up_16 = [b.bitcast(F16)[:, 0:MH * KT * P].rearrange("p (m k c) -> p m k c", m=MH, k=KT)
                 for b in (o_codes[:].rearrange("p h n -> p (h n)"), o_scale[:].rearrange("p h n -> p (h n)"))]

        def layernorm_dve(dve, n):
            def aggregate(t):
                dve.wait_ge(ln_bn, TT * n + t + 1)
                dve.bn_aggr(mv[:, t, :], bn[:, t, :]).then_inc(ln_mv, 1)

            for t in range(TT):
                if n == 0:
                    dve.wait_ge(d_x[t], 16)
                dve.bn_stats(bn[:, t, :], acc[:, t, :]).then_inc(ln_bn, 1)
                if t >= 1:
                    aggregate(t - 1)
            aggregate(TT - 1)
            dve.wait_ge(ln_mv, TT * n + TT)
            dve.tensor_scalar(ln[:, 0, :], mv[:, :, 1], EPS, None, ALU.add).then_inc(ln_var, 1)

        def rstd_dve(dve, n):
            v, root, y, a, b, c = (ln[:, i, :] for i in range(6))
            k = 5 * n
            dve.wait_ge(ln_sqrt, n + 1)
            dve.reciprocal(y, root).then_inc(ln_chain, 1)
            dve.wait_ge(ln_chain, k + 1)
            dve.tensor_tensor(a, y, y, ALU.mult).then_inc(ln_chain, 1)
            dve.wait_ge(ln_chain, k + 2)
            dve.tensor_tensor(b, a, v, ALU.mult).then_inc(ln_chain, 1)
            dve.wait_ge(ln_chain, k + 3)
            dve.tensor_scalar(c, b, -0.5, 1.5, ALU.mult, ALU.add).then_inc(ln_chain, 1)
            dve.wait_ge(ln_chain, k + 4)
            dve.tensor_tensor(a, y, c, ALU.mult).then_inc(ln_chain, 1)
            dve.wait_ge(ln_chain, k + 5)

        def layernorm_act(act, n):
            act.wait_ge(ln_var, n + 1)
            act.activation(ln[:, 1, :], ln[:, 0, :], ACT.Sqrt).then_inc(ln_sqrt, 1)

        def xn_dve(dve, n):
            def normalise(t):
                if t >= 2:
                    dve.wait_ge(ln_t, TT * n + t - 1)
                dve.tensor_scalar(rot[t % 2][:], acc[:, t, :], mv[:, t, 0:1], ln[:, 3, t:t + 1],
                                  ALU.subtract, ALU.mult).then_inc(ln_xn, 1)

            normalise(0)
            normalise(1)
            for t in range(TT):
                dve.wait_ge(ln_hi, TT * n + t + 1)
                hi, lo = xn_hi[:, :, t * P:(t + 1) * P], xn_lo[:, :, t * P:(t + 1) * P]
                dve.tensor_tensor(lo, ps_t[t % 2][:].rearrange("p (k c) -> p k c", k=KT), f(hi),
                                  ALU.subtract).then_inc(ln_lo, 1)
                if t + 2 < TT:
                    normalise(t + 2)

        def xn_act(act, n):
            for t in range(TT):
                act.wait_ge(ln_t, TT * n + t + 1)
                act.activation(xn_hi[:, :, t * P:(t + 1) * P], ps_t[t % 2][:].rearrange("p (k c) -> p k c", k=KT),
                               ACT.Copy).then_inc(ln_hi, 1)

        def xn_pe(pe, n):
            for t in range(TT):
                pe.wait_ge(ln_xn, TT * n + t + 1)
                if t >= 2:
                    pe.wait_ge(ln_lo, TT * n + t - 1)
                for k in range(KT):
                    last = pe.transpose(ps_t[t % 2][:, k * P:(k + 1) * P], rot[t % 2][:, k * P:(k + 1) * P], ident[:])
                last.then_inc(ln_t, 1)

        attn_scope = whole.enter_context(ExitStack())

        def sba(name, shape, dt):
            return sb(name, shape, dt, attn_scope)

        k_codes = sba("k_codes", [P, KT, P], I32)
        k_scale = sba("k_scale", [P, KT, P], F32)
        wq_hi = sba("wq_hi", [P, HPG, KT, P], F32R)
        wq_lo = sba("wq_lo", [P, HPG, KT, P], F32R)
        wk_hi = sba("wk_hi", [P, KT, P], F32R)
        wk_lo = sba("wk_lo", [P, KT, P], F32R)
        wo_hi = sba("wo_hi", [P, HPG, HID], F32R)
        wo_lo = sba("wo_lo", [P, HPG, HID], F32R)
        cos_sb = sba("cos_sb", [P, SEQ], F32)
        sin_sb = sba("sin_sb", [P, SEQ], F32)
        mask = sba("mask", [P, SEQ], F32)
        q_hi = sba("q_hi", [P, HPG, NHALF, HALF], F32R)
        q_lo = sba("q_lo", [P, HPG, NHALF, HALF], F32R)
        k_hi = sba("k_hi", [P, NHALF, HALF], F32R)
        k_lo = sba("k_lo", [P, NHALF, HALF], F32R)
        vg_hi = sba("vg_hi", [P, TT, P], F32R)
        vg_lo = sba("vg_lo", [P, TT, P], F32R)
        prob = [sba(f"prob{i}", [P, 2, TRI], F32) for i in range(2)]
        pt_hi = sba("pt_hi", [P, 2, TRI], F32R)
        pt_lo = sba("pt_lo", [P, 2, TRI], F32R)
        at_hi = sba("at_hi", [P, 2, HPG, SEQ], F32R)
        at_lo = sba("at_lo", [P, 2, HPG, SEQ], F32R)

        vw_codes = [q_codes[:].rearrange("p h k d -> p (h k d)"), o_codes[:].rearrange("p h n -> p (h n)")]
        vw_prods = [q_scale[:].rearrange("p h k d -> p (h k d)"), o_scale[:].rearrange("p h n -> p (h n)")]
        vw_hi_sb = [wq_hi[:].rearrange("p h k d -> p (h k d)"), at_hi[:].rearrange("p b h n -> p (b h n)")]
        vw_lo_sb = [wq_lo[:].rearrange("p h k d -> p (h k d)"), at_lo[:].rearrange("p b h n -> p (b h n)")]

        cols = [slice(0, P), slice(P, TRI)]

        def w_bufs(w):
            if w == 0:
                return k_codes[:], k_scale[:], wk_hi[:], wk_lo[:]
            return q_codes[:, w - 1], q_scale[:, w - 1], wq_hi[:, w - 1], wq_lo[:, w - 1]

        def u_bufs(half, w):
            if w == 0:
                return k_hi[:, half, :], k_lo[:, half, :]
            return q_hi[:, w - 1, half, :], q_lo[:, w - 1, half, :]

        def twice(table):
            return table[:].rearrange("p (a s) -> p a s", a=1).broadcast_to([P, 2, SEQ])

        def two(ap):
            return ap.rearrange("p (a s) -> p a s", a=2)

        def unit_slot(half, w):
            return (UNITS * half + w) % 2

        with nc.Block() as block:

            @block.sync
            def _(sp):
                for t in range(TT):
                    sp.dma_start(acc[:, t, :], x[t]).then_inc(d_x[t], 16)
                    if t == 1:
                        sp.dma_start(ident[:], eye).then_inc(d_const, 16)
                        sp.dma_start(vw_codes[0], vc[0]).then_inc(d_vw[0], 16)
                        sp.dma_start(vw_prods[0], vs[0].partition_broadcast(P)).then_inc(d_vw[0], 16)
                for dst, src in ((cos_sb, rope_cos), (sin_sb, rope_sin), (mask, causal)):
                    sp.dma_start(dst[:], src).then_inc(d_const, 16)
                sp.dma_start(vw_codes[1], vc[1]).then_inc(d_vw[1], 16)
                sp.dma_start(vw_prods[1], vs[1].partition_broadcast(P)).then_inc(d_vw[1], 16)

                def load_kq(g):
                    sp.dma_start(k_codes[:], kc[bass.ds(g, 1)].rearrange("g p k d -> (g p) k d")).then_inc(d_kw, 16)
                    sp.dma_start(k_scale[:].rearrange("p k d -> p (k d)"),
                                 ks[bass.ds(g, 1)].rearrange("g n -> (g n)").partition_broadcast(P)).then_inc(d_kw, 16)
                    sp.dma_start(q_codes[:], qc[bass.ds(g, 1)].rearrange("g p h k d -> (g p) h k d")).then_inc(d_qw, 16)
                    sp.dma_start(q_scale[:].rearrange("p h k d -> p (h k d)"),
                                 qs[bass.ds(g, 1)].rearrange("g n -> (g n)").partition_broadcast(P)).then_inc(d_qw, 16)

                def load_oc(g):
                    sp.dma_start(o_codes[:], oc[bass.ds(g, 1)].rearrange("g p h n -> (g p) h n")).then_inc(d_oc, 16)

                def load_os(g):
                    sp.dma_start(o_scale[:].rearrange("p h n -> p (h n)"),
                                 os_[bass.ds(g, 1)].rearrange("g n -> (g n)").partition_broadcast(P)).then_inc(d_os, 16)

                def load_v(g, b):
                    for dst, src in ((vg_hi, v_hi_d), (vg_lo, v_lo_d)):
                        sp.dma_start(f(dst[:, 2 * b:2 * b + 2, :]),
                                     src[bass.ds(g, 1), 2 * b:2 * b + 2].rearrange("g t p d -> p (g t) d")).then_inc(d_vin[b], 16)

                sp.wait_ge(vw_lo, 1)
                load_kq(0)
                sp.wait_ge(vw_lo, 2)
                load_oc(0)
                load_os(0)
                for n in range(2 * TT):
                    c, t = n // TT, n % TT
                    sp.wait_ge(v_lo, n + 1)
                    for src, dst in ((wo_hi, v_hi_d), (wo_lo, v_lo_d)):
                        sp.dma_start(dst[4 * c:4 * c + 4, t].rearrange("g p d -> p g d"),
                                     f(src[:, n % 4, :]).rearrange("p (g d) -> p g d", g=4)).then_inc(d_vout[n % 4], 16)
                for i in range(4):
                    sp.wait_ge(d_vout[i], 32 * 4)
                for b in range(BATCH):
                    load_v(0, b)

                def body(g, first, last):
                    if not last:
                        sp.wait_ge(w_lo, after_weight(g, UNITS - 1))
                        load_kq(g + 1)
                        sp.wait_ge(o_prod, HPG * g + HPG)
                        load_oc(g + 1)
                    if not first:
                        sp.wait_ge(pv_mm, after_step(g, 0) - 1)
                        load_v(g, BATCH - 1)
                    if not last:
                        sp.wait_ge(o_lo_p, 2 * g + 2)
                        sp.wait_ge(o_lo_v, 2 * g + 2)
                        load_os(g + 1)
                        for b in range(BATCH - 1):
                            sp.wait_ge(pv_mm, after_step(g, 2 * b + 1))
                            load_v(g + 1, b)

                groups(sp, body)
                sp.wait_ge(w_lo, after_weight(NKV - 1, UNITS - 1))
                for a in range(2):
                    sp.dma_start(gate_16[a].rearrange("p m k c -> p (m k c)"), wg[a]).then_inc(d_gu, 16)
                sp.wait_ge(o_lo_p, 2 * NKV)
                sp.wait_ge(o_lo_v, 2 * NKV)
                for a in range(2):
                    sp.dma_start(up_16[a].rearrange("p m k c -> p (m k c)"), wu[a]).then_inc(d_gu, 16)

            @block.scalar
            def _(act):
                def copy(out, in_):
                    return act.activation(out, in_, ACT.Copy)

                def unit_swap(g, half, w):
                    n = unit_slot(half, w)
                    act.wait_ge(u_mm, after_unit(g, half, w))
                    if earlier(g) or half or w >= 2:
                        act.wait_ge(u_lo, after_unit(g, half, w) - 2)
                    copy(rot[n][0:64, :], ps_unit[n][64:128, :]).then_inc(u_swap, 1)
                    copy(rot[n][64:128, :], ps_unit[n][0:64, :]).then_inc(u_swap, 1)

                def unit_hi(g, half, w):
                    hi, _ = u_bufs(half, w)
                    act.wait_ge(u_rot, after_unit(g, half, w))
                    if earlier(g):
                        act.wait_ge(s_mm, after_head(g - 1, 4 * half + 3, 1))
                    copy(hi, rot[unit_slot(half, w)][:]).then_inc(u_hi, 1)

                def weight_hi(g, w):
                    _, prod, hi, _ = w_bufs(w)
                    act.wait_ge(w_prod, after_weight(g, w))
                    if earlier(g):
                        act.wait_ge(u_mm, after_unit(g - 1, 1, w))
                    copy(hi, prod).then_inc(w_hi, 1)

                layernorm_act(act, 0)
                act.wait_ge(vw_prod, 1)
                copy(vw_hi_sb[0], vw_prods[0]).then_inc(vw_hi, 1)
                xn_act(act, 0)
                act.wait_ge(vw_prod, 2)
                copy(vw_hi_sb[1], vw_prods[1]).then_inc(vw_hi, 1)
                for n in range(2 * TT):
                    act.wait_ge(v_mm, n + 1)
                    if n >= 4:
                        act.wait_ge(d_vout[n % 4], 32 * (n // 4))
                    copy(wo_hi[:, n % 4, :], ps_unit[n % 2][:]).then_inc(v_hi, 1)
                    if n >= TT and n < TT + UNITS:
                        weight_hi(0, n - TT)
                for w in range(UNITS):
                    unit_swap(0, 0, w)
                    unit_hi(0, 0, w)

                def body(g, first, last):
                    pending = [] if first else [(0, 0, UNITS - 1)]
                    for s in range(STEPS + (3 if last else 0)):
                        if (not first or s >= 2) and s - 2 < STEPS:
                            act.wait_ge(pv_mm, after_step(g, s - 2))
                            if not first or s >= 6:
                                act.wait_ge(o_mm, after_out(g, (s - 2) // 2 - 2, 1))
                            copy(at_hi[:, ((s - 2) // 2) % 2, 2 * (s % 2):2 * (s % 2) + 2, :], two(ps_pv[:])).then_inc(pv_hi, 1)
                        if (not first or s >= 1) and s - 1 < STEPS:
                            for j in range(2):
                                act.wait_ge(t_mm, after_head(g, s - 1, j))
                                if not first or s >= 2:
                                    act.wait_ge(pv_mm, after_step(g, s - 2))
                                copy(pt_hi[:, j, :], ps_t[j][:, 0:TRI]).then_inc(t_hi, 1)
                        if s < STEPS:
                            for j in range(2):
                                act.wait_ge(s_neg, after_head(g, s, j))
                                for i in range(2):
                                    p = prob[s % 2][:, j, cols[i]]
                                    c = 2 * j + i
                                    act.activation(p, p, ACT.Exp, bias=nmax[:, s % 2, c:c + 1], scale=SCALE,
                                                   accum_out=rsum[:, s % 2, c:c + 1]).then_inc(s_exp, 1)
                        for dg, half, w in pending:
                            unit_hi(g + dg, half, w)
                        pending = units_of(s, last)
                        for w in weights_of(s, last):
                            weight_hi(g + 1, w)
                        if s == 2:
                            act.wait_ge(o_prod, HPG * g + HPG)
                            if first:
                                for i in range(4):
                                    act.wait_ge(d_vout[i], 32 * 4)
                            else:
                                act.wait_ge(o_mm, after_out(g - 1, BATCH - 1, 1))
                            for h in range(HPG):
                                copy(wo_hi[:, h, :], o_scale[:, h, :]).then_inc(o_hi, 1)
                        for dg, half, w in pending:
                            unit_swap(g + dg, half, w)

                groups(act, body)

            @block.vector
            def _(dve):
                def lo_part(out, full, hi):
                    return dve.tensor_tensor(out, full, f(hi), ALU.subtract)

                def product(codes, scale):
                    return dve.scalar_tensor_tensor(out=scale, in0=codes, scalar=OFFSET, in1=scale, op0=ALU.add, op1=ALU.mult)

                def weight_prod(g, w):
                    codes, scale, _, _ = w_bufs(w)
                    dve.wait_ge(d_kw if w == 0 else d_qw, 32 * (g + 1))
                    product(codes, scale).then_inc(w_prod, 1)

                def out_prod(g, h):
                    dve.wait_ge(d_oc, 16 * (g + 1))
                    dve.wait_ge(d_os, 16 * (g + 1))
                    product(o_codes[:, h, :], o_scale[:, h, :]).then_inc(o_prod, 1)

                def unit_rotate(g, half, w):
                    n = unit_slot(half, w)
                    dve.wait_ge(u_swap, 2 * after_unit(g, half, w))
                    if earlier(g) or half or w:
                        dve.wait_ge(u_rot, after_unit(g, half, w) - 1)
                    dve.tensor_tensor(two(rot_a[:]), two(ps_unit[n][:]), twice(cos_sb), ALU.mult).then_inc(u_cos, 1)
                    dve.wait_ge(u_cos, after_unit(g, half, w))
                    dve.wait_ge(u_sin, after_unit(g, half, w))
                    dve.tensor_tensor(rot[n][:], rot_a[:], rot[n][:], ALU.add).then_inc(u_rot, 1)

                layernorm_dve(dve, 0)
                dve.wait_ge(d_vw[0], 32)
                product(vw_codes[0], vw_prods[0]).then_inc(vw_prod, 1)
                rstd_dve(dve, 0)
                xn_dve(dve, 0)
                dve.wait_ge(d_vw[1], 32)
                product(vw_codes[1], vw_prods[1]).then_inc(vw_prod, 1)
                for n in range(2 * TT):
                    dve.wait_ge(v_hi, n + 1)
                    lo_part(wo_lo[:, n % 4, :], ps_unit[n % 2][:], wo_hi[:, n % 4, :]).then_inc(v_lo, 1)
                    if n < UNITS:
                        weight_prod(0, n)
                for h in range(HPG):
                    out_prod(0, h)
                dve.wait_ge(d_const, 4 * 16)
                for w in range(UNITS):
                    unit_rotate(0, 0, w)

                def add_out(g, b, i):
                    dve.wait_ge(o_mm, after_out(g, b, i))
                    tile = acc[:, (2 * b + i) % TT, :]
                    dve.tensor_tensor(tile, tile, ps_o[:], ALU.add).then_inc(o_add, 1)

                def body(g, first, last):
                    pending = [] if first else [(0, 0, UNITS - 1)]
                    for s in range(STEPS + (3 if last else 0)):
                        out_now = s % 2 == 0 and (not first or s >= 4)
                        if out_now:
                            add_out(g, s // 2 - 2, 0)
                        if (not first or s >= 2) and s - 2 < STEPS:
                            dve.wait_ge(pv_hi, after_step(g, s - 2))
                            at = ((s - 2) // 2) % 2, slice(2 * (s % 2), 2 * (s % 2) + 2)
                            lo_part(at_lo[:, at[0], at[1], :], two(ps_pv[:]), at_hi[:, at[0], at[1], :]).then_inc(pv_lo, 1)
                        if s < STEPS:
                            for j in range(2):
                                if not first or s >= 2:
                                    dve.wait_ge(t_mm, after_head(g, s - 2, j))
                                dve.wait_ge(s_mm, after_head(g, s, j))
                                dve.sem_inc(s_seen, 1)
                                for i in range(2):
                                    c = 2 * j + i
                                    dve.tensor_tensor_reduce(
                                        out=prob[s % 2][:, j, cols[i]], in0=ps_s[j][:, cols[i]],
                                        in1=mask[:, P:SEQ] if i == 0 else mask[:], scale=1.0, scalar=-3.4e38,
                                        op0=ALU.add, op1=ALU.max, accum_out=maxs[:, s % 2, c:c + 1]).then_inc(s_max, 1)
                            for j in range(2):
                                dve.wait_ge(s_max, after_tile(g, s, j, 1))
                                dve.tensor_scalar(nmax[:, s % 2, 2 * j:2 * j + 2], maxs[:, s % 2, 2 * j:2 * j + 2],
                                                  -SCALE, None, ALU.mult).then_inc(s_neg, 1)
                        if (not first or s >= 1) and s - 1 < STEPS:
                            for j in range(2):
                                dve.wait_ge(t_hi, after_head(g, s - 1, j))
                                lo_part(pt_lo[:, j, :], ps_t[j][:, 0:TRI], pt_hi[:, j, :]).then_inc(t_lo, 1)
                        if s == 3:
                            for h in (2, 3):
                                dve.wait_ge(o_hi, HPG * g + h + 1)
                                lo_part(wo_lo[:, h, :], o_scale[:, h, :], wo_hi[:, h, :]).then_inc(o_lo_v, 1)
                        for dg, half, w in pending:
                            unit_rotate(g + dg, half, w)
                        for w in weights_of(s, last):
                            weight_prod(g + 1, w)
                        if s in (6, 7) and not last:
                            for h in (2 * (s - 6), 2 * (s - 6) + 1):
                                out_prod(g + 1, h)
                        if s < STEPS:
                            for j in range(2):
                                dve.wait_ge(s_exp, after_tile(g, s, j, 1))
                                dve.reciprocal(rinv[:, s % 2, 2 * j:2 * j + 2], rsum[:, s % 2, 2 * j:2 * j + 2]).then_inc(s_inv, 1)
                            for j in range(2):
                                dve.wait_ge(s_inv, after_head(g, s, j))
                                for i in range(2):
                                    p = prob[s % 2][:, j, cols[i]]
                                    c = 2 * j + i
                                    dve.tensor_scalar(p, p, rinv[:, s % 2, c:c + 1], None, ALU.mult).then_inc(s_nrm, 1)
                        if out_now:
                            add_out(g, s // 2 - 2, 1)
                        units = units_of(s, last)
                        for dg, half, w in units[:-1]:
                            unit_rotate(g + dg, half, w)
                        pending = units[-1:]

                groups(dve, body)

            @block.gpsimd
            def _(pool):
                def lo_part(out, full, hi):
                    return pool.tensor_tensor(out, full, f(hi), ALU.subtract)

                def unit_sin(g, half, w):
                    n = unit_slot(half, w)
                    pool.wait_ge(u_swap, 2 * after_unit(g, half, w))
                    pool.tensor_tensor(two(rot[n][:]), two(rot[n][:]), twice(sin_sb), ALU.mult).then_inc(u_sin, 1)

                def unit_lo(g, half, w):
                    hi, lo = u_bufs(half, w)
                    pool.wait_ge(u_hi, after_unit(g, half, w))
                    lo_part(lo, rot[unit_slot(half, w)][:], hi).then_inc(u_lo, 1)

                def weight_lo(g, w):
                    _, prod, hi, lo = w_bufs(w)
                    pool.wait_ge(w_hi, after_weight(g, w))
                    lo_part(lo, prod, hi).then_inc(w_lo, 1)

                for c in range(2):
                    pool.wait_ge(vw_hi, c + 1)
                    lo_part(vw_lo_sb[c], vw_prods[c], vw_hi_sb[c]).then_inc(vw_lo, 1)
                for w in range(UNITS):
                    weight_lo(0, w)
                pool.wait_ge(d_const, 4 * 16)
                for w in range(UNITS):
                    unit_sin(0, 0, w)
                    unit_lo(0, 0, w)

                def body(g, first, last):
                    pending = [] if first else [(0, 0, UNITS - 1)]
                    for s in range(STEPS):
                        for dg, half, w in pending:
                            unit_lo(g + dg, half, w)
                        pending = units_of(s, last)
                        for w in weights_of(s, last):
                            weight_lo(g + 1, w)
                        if s == 2:
                            for h in (0, 1):
                                pool.wait_ge(o_hi, HPG * g + h + 1)
                                lo_part(wo_lo[:, h, :], o_scale[:, h, :], wo_hi[:, h, :]).then_inc(o_lo_p, 1)
                        for dg, half, w in pending:
                            unit_sin(g + dg, half, w)

                groups(pool, body)

            @block.tensor
            def _(pe):
                def three(out, a_hi, a_lo, b_hi, b_lo, first, last):
                    pe.matmul(out, a_hi, b_hi, start=first, stop=False)
                    pe.matmul(out, a_hi, b_lo, start=False, stop=False)
                    return pe.matmul(out, a_lo, b_hi, start=False, stop=last)

                def project(g, half, w):
                    _, _, hi, lo = w_bufs(w)
                    n = unit_slot(half, w)
                    pe.wait_ge(w_lo, after_weight(g, w))
                    if earlier(g) or half or w >= 2:
                        pe.wait_ge(u_cos, after_unit(g, half, w) - 2)
                    else:
                        pe.wait_ge(v_lo, 2 * TT - 1 + w)
                    for k in range(KT):
                        tokens = slice(half * HALF, (half + 1) * HALF)
                        mm = three(ps_unit[n][:], hi[:, k, :], lo[:, k, :], xn_hi[:, k, tokens], xn_lo[:, k, tokens],
                                   k == 0, k == KT - 1)
                    mm.then_inc(u_mm, 1)

                pe.wait_ge(d_const, 4 * 16)
                xn_pe(pe, 0)
                for n in range(2 * TT):
                    c, t = n // TT, n % TT
                    if c == 0:
                        pe.wait_ge(ln_lo, t + 1)
                    pe.wait_ge(vw_lo, c + 1)
                    if n >= 2:
                        pe.wait_ge(v_lo, n - 1)
                    for k in range(KT):
                        tok, wc = slice(t * P, (t + 1) * P), slice(k * HALF, (k + 1) * HALF)
                        mm = three(ps_unit[n % 2][:], xn_hi[:, k, tok], xn_lo[:, k, tok],
                                   vw_hi_sb[c][:, wc], vw_lo_sb[c][:, wc], k == 0, k == KT - 1)
                    mm.then_inc(v_mm, 1)
                for w in range(UNITS):
                    project(0, 0, w)

                def output(g, b, i):
                    pe.wait_ge(pv_lo, after_step(g, 2 * b + 1))
                    if not (isinstance(g, int) and g == 0 and b == 0 and i == 0):
                        pe.wait_ge(o_add, after_out(g, b, i) - 1)
                    gw = g if b >= 0 else g - 1
                    for h in range(HPG):
                        if h == 0:
                            pe.wait_ge(o_lo_p, 2 * gw + 2)
                        if h == 2:
                            pe.wait_ge(o_lo_v, 2 * gw + 2)
                        q = slice(i * P, (i + 1) * P)
                        mm = three(ps_o[:], at_hi[:, b % 2, h, q], at_lo[:, b % 2, h, q], wo_hi[:, h, :], wo_lo[:, h, :],
                                   h == 0, h == HPG - 1)
                    mm.then_inc(o_mm, 1)

                def scores(g, s, first):
                    b = s // 2
                    half, at = b // 2, (b % 2) * SEQ
                    for j in range(2):
                        h = 2 * (s % 2) + j
                        pe.wait_ge(u_lo, after_unit(g, half, 1 + h))
                        if not first or s >= 1:
                            pe.wait_ge(s_max, after_tile(g, s - 1, j, 1))
                        for i in range(2):
                            q, kk = slice(at + i * P, at + (i + 1) * P), slice(at, at + (i + 1) * P)
                            mm = three(ps_s[j][:, cols[i]], q_hi[:, h, half, q], q_lo[:, h, half, q],
                                       k_hi[:, half, kk], k_lo[:, half, kk], True, True)
                        mm.then_inc(s_mm, 1)

                def transposes(g, s, first):
                    for j in range(2):
                        pe.wait_ge(s_nrm, after_tile(g, s, j, 1))
                        if not first or s >= 1:
                            pe.wait_ge(t_lo, after_head(g, s - 1, j))
                        for n in range(3):
                            mm = pe.transpose(ps_t[j][:, n * P:(n + 1) * P], prob[s % 2][:, j, n * P:(n + 1) * P], ident[:])
                        mm.then_inc(t_mm, 1)

                def values(g, s, first):
                    b = s // 2
                    pe.wait_ge(d_vin[b], 32 * (g + 1))
                    pe.wait_ge(t_lo, after_head(g, s, 1))
                    if not first or s >= 1:
                        pe.wait_ge(pv_lo, after_step(g, s - 1))
                    for n in range(2):
                        out = ps_pv[:] if n == 0 else two(ps_pv[:])[:, :, P:SEQ]
                        kcols = slice(0, SEQ) if n == 0 else slice(SEQ, TRI)
                        if n == 0:
                            out = two(ps_pv[:])
                        mm = three(out, vg_hi[:, 2 * b + n, :], vg_lo[:, 2 * b + n, :],
                                   pt_hi[:, :, kcols], pt_lo[:, :, kcols], n == 0, n == 1)
                    mm.then_inc(pv_mm, 1)

                def body(g, first, last):
                    for s in range(STEPS + (3 if last else 0)):
                        if s < STEPS:
                            scores(g, s, first)
                        if (not first or s >= 1) and s - 1 < STEPS:
                            if s == 0:
                                transposes(g - 1, STEPS - 1, False)
                            else:
                                transposes(g, s - 1, first)
                        if s % 2 == 0 and (not first or s >= 4):
                            output(g, s // 2 - 2, 1)
                        for dg, half, w in units_of(s, last):
                            project(g + dg, half, w)
                        if (not first or s >= 1) and s - 1 < STEPS:
                            if s == 0:
                                values(g - 1, STEPS - 1, False)
                            else:
                                values(g, s - 1, first)
                        if s % 2 == 1 and (not first or s >= 3) and s - 3 < STEPS:
                            output(g, (s - 3) // 2, 0)

                groups(pe, body)

        attn_scope.close()

        gu_w = [sb(f"gu_w{i}", [P, 2, KT, P], F32R) for i in range(2)]
        wd_16 = sb("wd_16", [P, MT, HID], F16)
        wd_32 = sb("wd_32", [P, MT, HID], F32R)
        h_hi = sb("h_hi", [P, MT, HALF], F32R)
        h_lo = sb("h_lo", [P, MT, HALF], F32R)
        sg = [sb(f"sg{i}", [P, HALF], F32) for i in range(2)]
        hh = [sb(f"hh{i}", [P, HALF], F32) for i in range(2)]
        ps_gate, ps_up, ps_dn = ps_unit, ps_s, ps_t
        TH = TT // NHALF

        with nc.Block() as block:

            @block.sync
            def _(sp):
                sp.dma_start(wd_16[:], wd).then_inc(d_wd, 16)
                with sp.Fori(0, NHALF) as hf:
                    for i in range(TH):
                        sp.wait_ge(f_add, TH * hf + (i + 2))
                        sp.dma_start(out[bass.ds(TH * hf + i, 1)].rearrange("t p n -> (t p) n"),
                                     acc[:, bass.ds(TH * hf + i, 1), :].rearrange("p t n -> p (t n)")).then_inc(d_out, 16)
                sp.wait_ge(d_out, 16 * TT)

            @block.scalar
            def _(act):
                layernorm_act(act, 1)
                xn_act(act, 1)
                with act.Fori(0, NHALF) as hf:
                    def hidden_hi(m):
                        act.wait_ge(f_h, MT * hf + (m + 1))
                        if m == 0:
                            act.wait_ge(f_dn, TH * hf + 1)
                        act.activation(h_hi[:, m, :], hh[m % 2][:], ACT.Copy).then_inc(f_hi, 1)

                    for m in range(MT):
                        act.wait_ge(f_gu, 2 * MT * hf + (2 * m + 1))
                        if m >= 2:
                            act.wait_ge(f_h, MT * hf + (m - 1))
                        act.activation(sg[m % 2][:], ps_gate[m % 2][:], ACT.Silu).then_inc(f_sg, 1)
                        if m >= 1:
                            hidden_hi(m - 1)
                    hidden_hi(MT - 1)

            @block.vector
            def _(dve):
                dve.wait_ge(o_add, TT * NKV)
                layernorm_dve(dve, 1)
                rstd_dve(dve, 1)
                xn_dve(dve, 1)
                dve.wait_ge(d_gu, 4 * 16)
                dve.sem_inc(f_add, 1)
                with dve.Fori(0, NHALF) as hf:
                    def cast(m):
                        if m >= 2:
                            dve.wait_ge(f_gu, 2 * MT * hf + (2 * m - 2))
                        for n, w16 in enumerate((gate_16, up_16)):
                            dve.tensor_copy(gu_w[m % 2][:, n], w16[m // MH][:, m % MH]).then_inc(f_wcast, 1)

                    def hidden(m):
                        dve.wait_ge(f_sg, MT * hf + (m + 1))
                        dve.wait_ge(f_gu, 2 * MT * hf + (2 * m + 2))
                        if m >= 2:
                            dve.wait_ge(f_lo, MT * hf + (m - 1))
                        dve.tensor_tensor(hh[m % 2][:], sg[m % 2][:], ps_up[m % 2][:], ALU.mult).then_inc(f_h, 1)

                    def hidden_lo(m):
                        dve.wait_ge(f_hi, MT * hf + (m + 1))
                        dve.tensor_tensor(h_lo[:, m, :], hh[m % 2][:], f(h_hi[:, m, :]), ALU.subtract).then_inc(f_lo, 1)

                    cast(0)
                    for m in range(MT):
                        if m + 1 < MT:
                            cast(m + 1)
                        hidden(m)
                        if m >= 1:
                            hidden_lo(m - 1)
                    hidden_lo(MT - 1)
                    for i in range(TH):
                        dve.wait_ge(f_dn, TH * hf + (i + 2))
                        tile = acc[:, bass.ds(TH * hf + i, 1), :].rearrange("p t n -> p (t n)")
                        dve.tensor_tensor(tile, tile, ps_dn[i % 2][:], ALU.add).then_inc(f_add, 1)

            @block.gpsimd
            def _(pool):
                pool.wait_ge(d_wd, 16)
                for m in range(MT):
                    pool.tensor_scalar(wd_32[:, m, :], wd_16[:, m, :], 1.0, 1.0, ALU.mult, ALU.mult).then_inc(f_dcast, 1)

            @block.tensor
            def _(pe):
                xn_pe(pe, 1)
                pe.wait_ge(ln_lo, 2 * TT)
                pe.sem_inc(f_dn, 1)
                with pe.Fori(0, NHALF) as hf:
                    for m in range(MT):
                        for n, banks in enumerate((ps_gate, ps_up)):
                            pe.wait_ge(f_wcast, 2 * MT * hf + (2 * m + n + 1))
                            if m >= 2:
                                pe.wait_ge(f_h, MT * hf + (m - 1))
                            for k in range(KT):
                                for part in (xn_hi, xn_lo):
                                    mm = pe.matmul(banks[m % 2][:], gu_w[m % 2][:, n, k, :],
                                                   part[:, k, bass.ds(hf * HALF, HALF)],
                                                   start=(k == 0 and part is xn_hi), stop=(k == KT - 1 and part is xn_lo))
                            mm.then_inc(f_gu, 1)
                    pe.wait_ge(f_dcast, MT)
                    for i in range(TH):
                        pe.wait_ge(f_add, TH * hf + max(i, 1))
                        for m in range(MT):
                            if i == 0:
                                pe.wait_ge(f_lo, MT * hf + (m + 1))
                            for part in (h_hi, h_lo):
                                mm = pe.matmul(ps_dn[i % 2][:], part[:, m, i * P:(i + 1) * P], wd_32[:, m, :],
                                               start=(m == 0 and part is h_hi), stop=(m == MT - 1 and part is h_lo))
                        mm.then_inc(f_dn, 1)


def kernel(**inputs):
    import numpy as np
    import concourse.bacc as bacc
    from concourse.bass_utils import run_bass_kernel_spmd

    a = {n.removeprefix("L0_attn_").removeprefix("L0_ffn_"): np.asarray(v) for n, v in inputs.items()}

    def halves(w):
        return w.reshape(w.shape[0], -1, P // 2, 2).swapaxes(2, 3).reshape(w.shape)

    q_c = halves(a["q_codes"]).reshape(KT, P, NKV, HPG, P).transpose(2, 1, 3, 0, 4)
    q_s = halves(a["q_scales"]).reshape(KT, NKV, HPG, P).transpose(1, 2, 0, 3).reshape(NKV, -1)
    k_c = halves(a["k_codes"]).reshape(KT, P, NKV, P).transpose(2, 1, 0, 3)
    k_s = halves(a["k_scales"]).reshape(KT, NKV, P).transpose(1, 0, 2).reshape(NKV, -1)
    v_c = a["v_codes"].reshape(KT, P, 2, HALF).transpose(2, 1, 0, 3).reshape(2, P, -1)
    v_s = a["v_scales"].reshape(KT, 2, HALF).transpose(1, 0, 2).reshape(2, -1)
    o_c = a["o_codes"].reshape(NKV, HPG, P, HID).transpose(0, 2, 1, 3)
    o_s = a["o_scales"].reshape(NKV, -1)

    def ffn(w):
        return w.reshape(2, MH, P, KT, P).transpose(0, 4, 1, 3, 2).reshape(2, P, -1)

    w_d = a["W_down"].reshape(HID, MT, P).transpose(2, 1, 0)

    inv_freq = (1.0 / np.float32(10000.0) ** (np.arange(0, P, 2, dtype=np.float32) / np.float32(P))).astype(np.float32)
    angle = inv_freq[:, None] * np.arange(SEQ, dtype=np.float32)[None, :]
    cos = np.concatenate([np.cos(angle)] * 2).astype(np.float32)
    sin = np.concatenate([-np.sin(angle), np.sin(angle)]).astype(np.float32)
    mask = np.zeros((P, SEQ), np.float32)
    mask[:, P:] = np.where(np.arange(P)[None, :] <= np.arange(P)[:, None], 0.0, MASKED)

    arrays = {
        "x": a["hidden_states"].reshape(TT, P, HID), "qc": q_c, "qs": q_s, "kc": k_c, "ks": k_s, "vc": v_c, "vs": v_s,
        "oc": o_c, "os": o_s, "wg": ffn(a["W_gate"]), "wu": ffn(a["W_up"]), "wd": w_d,
        "rope_cos": cos, "rope_sin": sin, "causal": mask, "eye": np.eye(P, dtype=np.float32),
    }
    arrays = {n: np.ascontiguousarray(v) for n, v in arrays.items()}
    nc = bacc.Bacc("TRN2", target_bir_lowering=False, num_devices=1)
    args = [nc.dram_tensor(n, v.shape, mybir.dt.from_np(v.dtype), kind="ExternalInput").ap() for n, v in arrays.items()]
    y = nc.dram_tensor("y", (TT, P, HID), F32, kind="ExternalOutput").ap()
    layer_kernel(nc, *args, y)
    r = run_bass_kernel_spmd(nc, [arrays], core_ids=[0])
    return r.results[0]["y"].reshape(BATCH, SEQ, HID)
```

```python
from contextlib import ExitStack

import concourse.bass as bass
from concourse import mybir

F32 = mybir.dt.float32
F32R = mybir.dt.float32r
F16 = mybir.dt.float16
I32 = mybir.dt.int32
ALU = mybir.AluOpType
ACT = mybir.ActivationFunctionType

P = 128
BATCH, SEQ, HID = 4, 256, 512
TOK = BATCH * SEQ
TT = TOK // P
KT = HID // P
NH, NKV = 32, 8
HPG = NH // NKV
FFN = 1792
MT = FFN // P
MH = MT // 2
HALF = 512
NHALF = TOK // HALF
STEPS = 2 * BATCH
UNITS = 1 + HPG
TRI = P + SEQ
SCALE = P ** -0.5
EPS = 1e-5
OFFSET = -8.0
MASKED = -3.0e38


def f(ap):
    return ap.bitcast(F32)


def layer_kernel(nc, x, qc, qs, kc, ks, vc, vs, oc, os_, wg, wu, wd, rope_cos, rope_sin, causal, eye, out):
    v_hi_d = nc.dram_tensor("v_hi_scratch", (NKV, TT, P, P), F32, kind="Internal").ap()
    v_lo_d = nc.dram_tensor("v_lo_scratch", (NKV, TT, P, P), F32, kind="Internal").ap()

    with ExitStack() as whole:
        def sem(name):
            return whole.enter_context(nc.semaphore(name))

        def sb(name, shape, dt, ctx=whole):
            return ctx.enter_context(nc.sbuf_tensor(name, shape, dt))

        def bank(name):
            return whole.enter_context(nc.psum_tensor(name, [P, HALF], F32))

        ps_unit = [bank(f"ps_unit{i}") for i in range(2)]
        ps_s = [bank(f"ps_s{i}") for i in range(2)]
        ps_t = [bank(f"ps_t{i}") for i in range(2)]
        ps_pv = bank("ps_pv")
        ps_o = bank("ps_o")

        acc = sb("acc", [P, TT, HID], F32)
        xn_hi = sb("xn_hi", [P, KT, TOK], F32R)
        xn_lo = sb("xn_lo", [P, KT, TOK], F32R)
        rot = [sb(f"rot{i}", [P, HALF], F32) for i in range(2)]
        rot_a = sb("rot_a", [P, HALF], F32)
        k_codes = sb("k_codes", [P, KT, P], I32)
        k_scale = sb("k_scale", [P, KT, P], F32)
        wq_hi = sb("wq_hi", [P, HPG, KT, P], F32R)
        ident = sb("ident", [P, P], F32)
        bn = sb("bn", [P, TT, 6], F32)
        mv = sb("mv", [P, TT, 2], F32)
        ln = sb("ln", [P, 6, TT], F32)
        maxs = sb("maxs", [P, 2, 4], F32)
        nmax = sb("nmax", [P, 2, 4], F32)
        rsum = sb("rsum", [P, 2, 4], F32)
        rinv = sb("rinv", [P, 2, 4], F32)

        d_x = [sem(f"d_x{t}") for t in range(TT)]
        d_id, d_const = sem("d_id"), sem("d_const")
        d_vw = [sem(f"d_vw{c}") for c in range(2)]
        d_vout = [sem(f"d_vout{i}") for i in range(4)]
        d_vin = [sem(f"d_vin{b}") for b in range(BATCH)]
        d_kw, d_qw, d_oc, d_os = sem("d_kw"), sem("d_qw"), sem("d_oc"), sem("d_os")
        d_gu, d_wd = sem("d_gu"), sem("d_wd")
        d_out = sem("d_out")
        ln_bn, ln_mv, ln_var, ln_sqrt, ln_chain = sem("ln_bn"), sem("ln_mv"), sem("ln_var"), sem("ln_sqrt"), sem("ln_chain")
        ln_xn, ln_t, ln_hi, ln_lo = sem("ln_xn"), sem("ln_t"), sem("ln_hi"), sem("ln_lo")
        vw_prod, vw_hi, vw_lo = sem("vw_prod"), sem("vw_hi"), sem("vw_lo")
        v_mm, v_hi, v_lo = sem("v_mm"), sem("v_hi"), sem("v_lo")
        w_prod, w_hi, w_lo = sem("w_prod"), sem("w_hi"), sem("w_lo")
        o_prod, o_hi, o_lo_p, o_lo_v = sem("o_prod"), sem("o_hi"), sem("o_lo_p"), sem("o_lo_v")
        u_mm, u_swap, u_cos, u_sin, u_rot, u_hi, u_lo = (sem(n) for n in ("u_mm", "u_swap", "u_cos", "u_sin", "u_rot", "u_hi", "u_lo"))
        s_mm, s_max, s_neg, s_exp, s_inv, s_nrm = (sem(n) for n in ("s_mm", "s_max", "s_neg", "s_exp", "s_inv", "s_nrm"))
        s_seen = sem("s_seen")
        t_mm, t_hi, t_lo = sem("t_mm"), sem("t_hi"), sem("t_lo")
        pv_mm, pv_hi, pv_lo = sem("pv_mm"), sem("pv_hi"), sem("pv_lo")
        o_mm, o_add = sem("o_mm"), sem("o_add")
        f_wcast, f_gu, f_sg, f_h, f_hi, f_lo, f_dcast, f_dn, f_add = (
            sem(n) for n in ("f_wcast", "f_gu", "f_sg", "f_h", "f_hi", "f_lo", "f_dcast", "f_dn", "f_add"))

        def after_head(g, s, j):
            return 2 * STEPS * g + (2 * s + j + 1)

        def after_tile(g, s, j, i):
            return 4 * STEPS * g + (4 * s + 2 * j + i + 1)

        def after_step(g, s):
            return STEPS * g + (s + 1)

        def after_unit(g, half, w):
            return 2 * UNITS * g + (UNITS * half + w + 1)

        def after_weight(g, w):
            return UNITS * g + (w + 1)

        def after_out(g, b, i):
            return TT * g + (2 * b + i + 1)

        def units_of(s, last):
            if s >= STEPS:
                return []
            if s < 4:
                return ([(0, 1, 0)] if s == 0 else []) + [(0, 1, 1 + s)]
            return [] if last else ([(1, 0, 0)] if s == 4 else []) + [(1, 0, 1 + s - 4)]

        def weights_of(s, last):
            return [] if last else {1: [0], 3: [1], 4: [2], 5: [3], 6: [4]}.get(s, [])

        def groups(eng, body):
            body(0, True, False)
            with eng.Fori(1, NKV - 1) as g:
                body(g, False, False)
            body(NKV - 1, False, True)

        def earlier(g):
            return not (isinstance(g, int) and g == 0)

        q_codes = sb("q_codes", [P, HPG, KT, P], I32)
        q_scale = sb("q_scale", [P, HPG, KT, P], F32)
        o_codes = sb("o_codes", [P, HPG, HID], I32)
        o_scale = sb("o_scale", [P, HPG, HID], F32)
        gate_16 = [b.bitcast(F16)[:, 0:MH * KT * P].rearrange("p (m k c) -> p m k c", m=MH, k=KT)
                   for b in (q_codes[:].rearrange("p h k d -> p (h k d)"), q_scale[:].rearrange("p h k d -> p (h k d)"))]
        up_16 = [b.bitcast(F16)[:, 0:MH * KT * P].rearrange("p (m k c) -> p m k c", m=MH, k=KT)
                 for b in (o_codes[:].rearrange("p h n -> p (h n)"), o_scale[:].rearrange("p h n -> p (h n)"))]

        gu_w = [wq_hi[:, 2 * i:2 * i + 2] for i in range(2)]
        k_scale_row = k_scale[:].rearrange("p k d -> p (k d)")
        rows_2 = [rot[0][:], rot[1][:], rot_a[:], k_scale_row]
        four_banks = ps_t + [ps_pv, ps_o]

        TP = TT // 2

        def tiles(part):
            return range(TP * part, TP * part + TP)

        def stats_dve(dve, n, part):
            def aggregate(t):
                dve.wait_ge(ln_bn, TT * n + t + 1)
                dve.bn_aggr(mv[:, t, :], bn[:, t, :]).then_inc(ln_mv, 1)

            for t in tiles(part):
                if n == 0:
                    dve.wait_ge(d_x[t], 16)
                dve.bn_stats(bn[:, t, :], acc[:, t, :]).then_inc(ln_bn, 1)
                if t > TP * part:
                    aggregate(t - 1)
            aggregate(TP * part + TP - 1)
            dve.wait_ge(ln_mv, TT * n + TP * part + TP)
            dve.tensor_scalar(ln[:, 0, TP * part:TP * part + TP], mv[:, TP * part:TP * part + TP, 1], EPS, None,
                              ALU.add).then_inc(ln_var, 1)

        def sqrt_act(act, n, part):
            act.wait_ge(ln_var, 2 * n + part + 1)
            own = slice(TP * part, TP * part + TP)
            act.activation(ln[:, 1, own], ln[:, 0, own], ACT.Sqrt).then_inc(ln_sqrt, 1)

        def rstd_dve(dve, n, part):
            v, root, y, a, b, c = (ln[:, i, TP * part:TP * part + TP] for i in range(6))
            k = 5 * (2 * n + part)
            dve.wait_ge(ln_sqrt, 2 * n + part + 1)
            dve.reciprocal(y, root).then_inc(ln_chain, 1)
            dve.wait_ge(ln_chain, k + 1)
            dve.tensor_tensor(a, y, y, ALU.mult).then_inc(ln_chain, 1)
            dve.wait_ge(ln_chain, k + 2)
            dve.tensor_tensor(b, a, v, ALU.mult).then_inc(ln_chain, 1)
            dve.wait_ge(ln_chain, k + 3)
            dve.tensor_scalar(c, b, -0.5, 1.5, ALU.mult, ALU.add).then_inc(ln_chain, 1)
            dve.wait_ge(ln_chain, k + 4)
            dve.tensor_tensor(a, y, c, ALU.mult).then_inc(ln_chain, 1)
            dve.wait_ge(ln_chain, k + 5)

        def normalise_dve(dve, n, t, rows):
            if t >= len(rows):
                dve.wait_ge(ln_t, TT * n + t - len(rows) + 1)
            dve.tensor_scalar(rows[t % len(rows)], acc[:, t, :], mv[:, t, 0:1], ln[:, 3, t:t + 1],
                              ALU.subtract, ALU.mult).then_inc(ln_xn, 1)

        def normalise_tiles(dve, n, part, rows):
            for t in tiles(part):
                normalise_dve(dve, n, t, rows)

        def xn_lo_dve(dve, n, part, banks):
            for t in tiles(part):
                dve.wait_ge(ln_hi, TT * n + t + 1)
                hi, lo = xn_hi[:, :, t * P:(t + 1) * P], xn_lo[:, :, t * P:(t + 1) * P]
                dve.tensor_tensor(lo, banks[t % len(banks)][:].rearrange("p (k c) -> p k c", k=KT), f(hi),
                                  ALU.subtract).then_inc(ln_lo, 1)

        def xn_hi_act(act, n, part, banks):
            for t in tiles(part):
                act.wait_ge(ln_t, TT * n + t + 1)
                act.activation(xn_hi[:, :, t * P:(t + 1) * P],
                               banks[t % len(banks)][:].rearrange("p (k c) -> p k c", k=KT), ACT.Copy).then_inc(ln_hi, 1)

        def xn_pe(pe, n, part, rows, banks):
            for t in tiles(part):
                pe.wait_ge(ln_xn, TT * n + t + 1)
                if t >= len(banks):
                    pe.wait_ge(ln_lo, TT * n + t - len(banks) + 1)
                for k in range(KT):
                    last = pe.transpose(banks[t % len(banks)][:, k * P:(k + 1) * P],
                                        rows[t % len(rows)][:, k * P:(k + 1) * P], ident[:])
                last.then_inc(ln_t, 1)

        ps_gate, ps_up, ps_dn = ps_unit, ps_s, ps_t

        def gate_up_cast(pool, n):
            for a, w16 in enumerate((gate_16, up_16)):
                pool.tensor_scalar(gu_w[n % 2][:, a], w16[n % MT // MH][:, n % MT % MH], 1.0, 1.0,
                                   ALU.mult, ALU.mult).then_inc(f_wcast, 1)

        def gate_up(pe, n):
            half = slice(n // MT * HALF, (n // MT + 1) * HALF)
            for a, banks in enumerate((ps_gate, ps_up)):
                pe.wait_ge(f_wcast, 2 * n + a + 1)
                if n % MT == 0:
                    pe.wait_ge(ln_lo, TT + TP * (n // MT + 1))
                if n >= 2:
                    pe.wait_ge(f_h, n - 1)
                for k in range(KT):
                    for part in (xn_hi, xn_lo):
                        mm = pe.matmul(banks[n % 2][:], gu_w[n % 2][:, a, k, :], part[:, k, half],
                                       start=(k == 0 and part is xn_hi), stop=(k == KT - 1 and part is xn_lo))
                mm.then_inc(f_gu, 1)

        attn_scope = whole.enter_context(ExitStack())

        def sba(name, shape, dt):
            return sb(name, shape, dt, attn_scope)

        wq_lo = sba("wq_lo", [P, HPG, KT, P], F32R)
        wk_hi = sba("wk_hi", [P, KT, P], F32R)
        wk_lo = sba("wk_lo", [P, KT, P], F32R)
        wo_hi = sba("wo_hi", [P, HPG, HID], F32R)
        wo_lo = sba("wo_lo", [P, HPG, HID], F32R)
        cos_sb = sba("cos_sb", [P, SEQ], F32)
        sin_sb = sba("sin_sb", [P, SEQ], F32)
        mask = sba("mask", [P, SEQ], F32)
        q_hi = sba("q_hi", [P, HPG, NHALF, HALF], F32R)
        q_lo = sba("q_lo", [P, HPG, NHALF, HALF], F32R)
        k_hi = sba("k_hi", [P, NHALF, HALF], F32R)
        k_lo = sba("k_lo", [P, NHALF, HALF], F32R)
        vg_hi = sba("vg_hi", [P, TT, P], F32R)
        vg_lo = sba("vg_lo", [P, TT, P], F32R)
        prob = [sba(f"prob{i}", [P, 2, TRI], F32) for i in range(2)]
        pt_hi = sba("pt_hi", [P, 2, TRI], F32R)
        pt_lo = sba("pt_lo", [P, 2, TRI], F32R)
        at_hi = sba("at_hi", [P, 2, HPG, SEQ], F32R)
        at_lo = sba("at_lo", [P, 2, HPG, SEQ], F32R)

        vw_codes = [o_codes[:].rearrange("p h n -> p (h n)"), q_codes[:].rearrange("p h k d -> p (h k d)")]
        vw_prods = [o_scale[:].rearrange("p h n -> p (h n)"), q_scale[:].rearrange("p h k d -> p (h k d)")]
        vw_hi_sb = [at_hi[:].rearrange("p b h n -> p (b h n)"), wo_hi[:].rearrange("p h n -> p (h n)")]
        vw_lo_sb = [at_lo[:].rearrange("p b h n -> p (b h n)"), wo_lo[:].rearrange("p h n -> p (h n)")]
        v_out_hi = [q_hi[:, i, 1, :] for i in range(4)]
        v_out_lo = [q_lo[:, i, 1, :] for i in range(4)]
        prob_rows = [p[:].rearrange("p j c -> p (j c)")[:, 0:HID] for p in prob]
        rows_1 = [prob_rows + [rot[0][:], rot[1][:]],
                  prob_rows + [k_codes[:].bitcast(F32).rearrange("p k d -> p (k d)"), k_scale_row]]

        def vw_cols(k):
            return slice(k * HALF, (k + 1) * HALF)

        cols = [slice(0, P), slice(P, TRI)]

        def w_bufs(w):
            if w == 0:
                return k_codes[:], k_scale[:], wk_hi[:], wk_lo[:]
            return q_codes[:, w - 1], q_scale[:, w - 1], wq_hi[:, w - 1], wq_lo[:, w - 1]

        def u_bufs(half, w):
            if w == 0:
                return k_hi[:, half, :], k_lo[:, half, :]
            return q_hi[:, w - 1, half, :], q_lo[:, w - 1, half, :]

        def twice(table):
            return table[:].rearrange("p (a s) -> p a s", a=1).broadcast_to([P, 2, SEQ])

        def two(ap):
            return ap.rearrange("p (a s) -> p a s", a=2)

        def unit_slot(half, w):
            return (UNITS * half + w) % 2

        with nc.Block() as block:

            @block.sync
            def _(sp):
                def load_x(part):
                    for t in tiles(part):
                        sp.dma_start(acc[:, t, :], x[t]).then_inc(d_x[t], 16)

                def load_kq(g):
                    sp.dma_start(k_codes[:], kc[bass.ds(g, 1)].rearrange("g p k d -> (g p) k d")).then_inc(d_kw, 16)
                    sp.dma_start(k_scale[:].rearrange("p k d -> p (k d)"),
                                 ks[bass.ds(g, 1)].rearrange("g n -> (g n)").partition_broadcast(P)).then_inc(d_kw, 16)
                    sp.dma_start(q_codes[:], qc[bass.ds(g, 1)].rearrange("g p h k d -> (g p) h k d")).then_inc(d_qw, 16)
                    sp.dma_start(q_scale[:].rearrange("p h k d -> p (h k d)"),
                                 qs[bass.ds(g, 1)].rearrange("g n -> (g n)").partition_broadcast(P)).then_inc(d_qw, 16)

                def load_oc(g):
                    sp.dma_start(o_codes[:], oc[bass.ds(g, 1)].rearrange("g p h n -> (g p) h n")).then_inc(d_oc, 16)

                def load_os(g):
                    sp.dma_start(o_scale[:].rearrange("p h n -> p (h n)"),
                                 os_[bass.ds(g, 1)].rearrange("g n -> (g n)").partition_broadcast(P)).then_inc(d_os, 16)

                def load_v(g, b):
                    for dst, src in ((vg_hi, v_hi_d), (vg_lo, v_lo_d)):
                        sp.dma_start(f(dst[:, 2 * b:2 * b + 2, :]),
                                     src[bass.ds(g, 1), 2 * b:2 * b + 2].rearrange("g t p d -> p (g t) d")).then_inc(d_vin[b], 16)

                def load_vw(c):
                    sp.dma_start(vw_codes[c], vc[c]).then_inc(d_vw[c], 16)
                    sp.dma_start(vw_prods[c], vs[c].partition_broadcast(P)).then_inc(d_vw[c], 16)

                load_x(0)
                sp.dma_start(ident[:], eye).then_inc(d_id, 16)
                load_kq(0)
                load_x(1)
                for dst, src in ((cos_sb, rope_cos), (sin_sb, rope_sin), (mask, causal)):
                    sp.dma_start(dst[:], src).then_inc(d_const, 16)
                load_vw(0)
                sp.wait_ge(w_lo, UNITS)
                load_vw(1)
                sp.wait_ge(vw_lo, KT)
                load_oc(0)
                load_os(0)
                for n in range(2 * TT):
                    c, t = n // TT, n % TT
                    if n == TT:
                        for i in range(4):
                            sp.wait_ge(d_vout[i], 32 * 2)
                        for b in range(BATCH):
                            load_v(0, b)
                    sp.wait_ge(v_lo, n + 1)
                    for src, dst in ((v_out_hi, v_hi_d), (v_out_lo, v_lo_d)):
                        sp.dma_start(dst[4 * c:4 * c + 4, t].rearrange("g p d -> p g d"),
                                     f(src[n % 4]).rearrange("p (g d) -> p g d", g=4)).then_inc(d_vout[n % 4], 16)
                for i in range(4):
                    sp.wait_ge(d_vout[i], 32 * 4)

                def body(g, first, last):
                    if not last:
                        sp.wait_ge(w_lo, after_weight(g, UNITS - 1))
                        load_kq(g + 1)
                        sp.wait_ge(o_prod, HPG * g + HPG)
                        load_oc(g + 1)
                    if not first:
                        sp.wait_ge(pv_mm, after_step(g, 0) - 1)
                        load_v(g, BATCH - 1)
                    if not last:
                        sp.wait_ge(o_lo_p, 2 * g + 2)
                        sp.wait_ge(o_lo_v, 2 * g + 2)
                        load_os(g + 1)
                        for b in range(BATCH - 1):
                            sp.wait_ge(pv_mm, after_step(g, 2 * b + 1))
                            load_v(g + 1, b)

                groups(sp, body)
                sp.wait_ge(w_lo, after_weight(NKV - 1, UNITS - 1))
                for a in range(2):
                    sp.dma_start(gate_16[a].rearrange("p m k c -> p (m k c)"), wg[a]).then_inc(d_gu, 16)
                sp.wait_ge(o_lo_p, 2 * NKV)
                sp.wait_ge(o_lo_v, 2 * NKV)
                for a in range(2):
                    sp.dma_start(up_16[a].rearrange("p m k c -> p (m k c)"), wu[a]).then_inc(d_gu, 16)

            @block.scalar
            def _(act):
                def copy(out, in_):
                    return act.activation(out, in_, ACT.Copy)

                def unit_swap(g, half, w):
                    n = unit_slot(half, w)
                    act.wait_ge(u_mm, after_unit(g, half, w))
                    if earlier(g) or half or w >= 2:
                        act.wait_ge(u_lo, after_unit(g, half, w) - 2)
                    copy(rot[n][0:64, :], ps_unit[n][64:128, :]).then_inc(u_swap, 1)
                    copy(rot[n][64:128, :], ps_unit[n][0:64, :]).then_inc(u_swap, 1)

                def unit_hi(g, half, w):
                    hi, _ = u_bufs(half, w)
                    act.wait_ge(u_rot, after_unit(g, half, w))
                    if earlier(g):
                        act.wait_ge(s_mm, after_head(g - 1, 4 * half + 3, 1))
                    elif half and w:
                        act.wait_ge(d_vout[w - 1], 32 * 4)
                    copy(hi, rot[unit_slot(half, w)][:]).then_inc(u_hi, 1)

                def weight_hi(g, w):
                    _, prod, hi, _ = w_bufs(w)
                    act.wait_ge(w_prod, after_weight(g, w))
                    if earlier(g):
                        act.wait_ge(u_mm, after_unit(g - 1, 1, w))
                    copy(hi, prod).then_inc(w_hi, 1)

                def v_weights_hi(c):
                    for k in range(KT):
                        act.wait_ge(vw_prod, KT * c + k + 1)
                        copy(vw_hi_sb[c][:, vw_cols(k)], vw_prods[c][:, vw_cols(k)]).then_inc(vw_hi, 1)

                sqrt_act(act, 0, 0)
                xn_hi_act(act, 0, 0, four_banks)
                for w in range(3):
                    weight_hi(0, w)
                unit_swap(0, 0, 0)
                weight_hi(0, 3)
                sqrt_act(act, 0, 1)
                unit_swap(0, 0, 1)
                unit_hi(0, 0, 0)
                weight_hi(0, 4)
                xn_hi_act(act, 0, 1, four_banks)
                unit_hi(0, 0, 1)
                unit_swap(0, 0, 2)
                v_weights_hi(0)
                unit_hi(0, 0, 2)
                unit_swap(0, 0, 3)
                unit_hi(0, 0, 3)
                unit_swap(0, 0, 4)
                unit_hi(0, 0, 4)
                for n in range(2 * TT):
                    if n == 3:
                        v_weights_hi(1)
                    act.wait_ge(v_mm, n + 1)
                    if n >= 4:
                        act.wait_ge(d_vout[n % 4], 32 * (n // 4))
                    copy(v_out_hi[n % 4], ps_s[n % 2][:]).then_inc(v_hi, 1)

                def body(g, first, last):
                    pending = [] if first else [(0, 0, UNITS - 1)]
                    for s in range(STEPS + (3 if last else 0)):
                        if (not first or s >= 2) and s - 2 < STEPS:
                            act.wait_ge(pv_mm, after_step(g, s - 2))
                            if not first or s >= 6:
                                act.wait_ge(o_mm, after_out(g, (s - 2) // 2 - 2, 1))
                            copy(at_hi[:, ((s - 2) // 2) % 2, 2 * (s % 2):2 * (s % 2) + 2, :], two(ps_pv[:])).then_inc(pv_hi, 1)
                        if last and s == STEPS:
                            sqrt_act(act, 1, 0)
                        if last and s == STEPS + 1:
                            xn_hi_act(act, 1, 0, ps_unit)
                        if (not first or s >= 1) and s - 1 < STEPS:
                            for j in range(2):
                                act.wait_ge(t_mm, after_head(g, s - 1, j))
                                if not first or s >= 2:
                                    act.wait_ge(pv_mm, after_step(g, s - 2))
                                copy(pt_hi[:, j, :], ps_t[j][:, 0:TRI]).then_inc(t_hi, 1)
                        if s < STEPS:
                            for j in range(2):
                                act.wait_ge(s_neg, after_head(g, s, j))
                                for i in range(2):
                                    p = prob[s % 2][:, j, cols[i]]
                                    c = 2 * j + i
                                    act.activation(p, p, ACT.Exp, bias=nmax[:, s % 2, c:c + 1], scale=SCALE,
                                                   accum_out=rsum[:, s % 2, c:c + 1]).then_inc(s_exp, 1)
                        for dg, half, w in pending:
                            unit_hi(g + dg, half, w)
                        pending = units_of(s, last)
                        for w in weights_of(s, last):
                            weight_hi(g + 1, w)
                        if s == 2:
                            act.wait_ge(o_prod, HPG * g + HPG)
                            if not first:
                                act.wait_ge(o_mm, after_out(g - 1, BATCH - 1, 1))
                            for h in range(HPG):
                                copy(wo_hi[:, h, :], o_scale[:, h, :]).then_inc(o_hi, 1)
                        for dg, half, w in pending:
                            unit_swap(g + dg, half, w)

                groups(act, body)

            @block.vector
            def _(dve):
                def lo_part(out, full, hi):
                    return dve.tensor_tensor(out, full, f(hi), ALU.subtract)

                def product(codes, scale):
                    return dve.scalar_tensor_tensor(out=scale, in0=codes, scalar=OFFSET, in1=scale, op0=ALU.add, op1=ALU.mult)

                def weight_prod(g, w):
                    codes, scale, _, _ = w_bufs(w)
                    dve.wait_ge(d_kw if w == 0 else d_qw, 32 * (g + 1))
                    product(codes, scale).then_inc(w_prod, 1)

                def out_prod(g, h):
                    dve.wait_ge(d_oc, 16 * (g + 1))
                    dve.wait_ge(d_os, 16 * (g + 1))
                    product(o_codes[:, h, :], o_scale[:, h, :]).then_inc(o_prod, 1)

                def unit_cos(g, half, w):
                    n = unit_slot(half, w)
                    dve.wait_ge(u_swap, 2 * after_unit(g, half, w))
                    if earlier(g) or half or w:
                        dve.wait_ge(u_rot, after_unit(g, half, w) - 1)
                    dve.tensor_tensor(two(rot_a[:]), two(ps_unit[n][:]), twice(cos_sb), ALU.mult).then_inc(u_cos, 1)

                def unit_add(g, half, w):
                    n = unit_slot(half, w)
                    dve.wait_ge(u_cos, after_unit(g, half, w))
                    dve.wait_ge(u_sin, after_unit(g, half, w))
                    dve.tensor_tensor(rot[n][:], rot_a[:], rot[n][:], ALU.add).then_inc(u_rot, 1)

                def unit_rotate(g, half, w):
                    unit_cos(g, half, w)
                    unit_add(g, half, w)

                def v_weights(c):
                    dve.wait_ge(d_vw[c], 32)
                    for k in range(KT):
                        product(vw_codes[c][:, vw_cols(k)], vw_prods[c][:, vw_cols(k)]).then_inc(vw_prod, 1)

                def v_weights_lo(c):
                    for k in range(KT):
                        dve.wait_ge(vw_hi, KT * c + k + 1)
                        lo_part(vw_lo_sb[c][:, vw_cols(k)], vw_prods[c][:, vw_cols(k)], vw_hi_sb[c][:, vw_cols(k)]).then_inc(vw_lo, 1)

                stats_dve(dve, 0, 0)
                rstd_dve(dve, 0, 0)
                normalise_tiles(dve, 0, 0, rows_1[0])
                weight_prod(0, 0)
                xn_lo_dve(dve, 0, 0, four_banks)
                for w in (1, 2, 3):
                    weight_prod(0, w)
                stats_dve(dve, 0, 1)
                dve.wait_ge(d_const, 3 * 16)
                unit_cos(0, 0, 0)
                rstd_dve(dve, 0, 1)
                dve.wait_ge(w_lo, 1)
                normalise_tiles(dve, 0, 1, rows_1[1])
                unit_add(0, 0, 0)
                unit_cos(0, 0, 1)
                weight_prod(0, 4)
                unit_add(0, 0, 1)
                xn_lo_dve(dve, 0, 1, four_banks)
                unit_cos(0, 0, 2)
                v_weights(0)
                unit_add(0, 0, 2)
                v_weights_lo(0)
                unit_rotate(0, 0, 3)
                unit_rotate(0, 0, 4)
                for n in range(2 * TT):
                    if n == 3:
                        v_weights(1)
                        v_weights_lo(1)
                    dve.wait_ge(v_hi, n + 1)
                    lo_part(v_out_lo[n % 4], ps_s[n % 2][:], v_out_hi[n % 4]).then_inc(v_lo, 1)
                for h in range(HPG):
                    out_prod(0, h)

                def add_out(g, b, i):
                    dve.wait_ge(o_mm, after_out(g, b, i))
                    tile = acc[:, (2 * b + i) % TT, :]
                    dve.tensor_tensor(tile, tile, ps_o[:], ALU.add).then_inc(o_add, 1)

                def body(g, first, last):
                    pending = [] if first else [(0, 0, UNITS - 1)]
                    for s in range(STEPS + (3 if last else 0)):
                        out_now = s % 2 == 0 and (not first or s >= 4)
                        if out_now:
                            add_out(g, s // 2 - 2, 0)
                        if (not first or s >= 2) and s - 2 < STEPS:
                            dve.wait_ge(pv_hi, after_step(g, s - 2))
                            at = ((s - 2) // 2) % 2, slice(2 * (s % 2), 2 * (s % 2) + 2)
                            lo_part(at_lo[:, at[0], at[1], :], two(ps_pv[:]), at_hi[:, at[0], at[1], :]).then_inc(pv_lo, 1)
                        if last and s == STEPS + 1:
                            xn_lo_dve(dve, 1, 0, ps_unit)
                        if s < STEPS:
                            for j in range(2):
                                if not first or s >= 2:
                                    dve.wait_ge(t_mm, after_head(g, s - 2, j))
                                dve.wait_ge(s_mm, after_head(g, s, j))
                                dve.sem_inc(s_seen, 1)
                                for i in range(2):
                                    c = 2 * j + i
                                    dve.tensor_tensor_reduce(
                                        out=prob[s % 2][:, j, cols[i]], in0=ps_s[j][:, cols[i]],
                                        in1=mask[:, P:SEQ] if i == 0 else mask[:], scale=1.0, scalar=-3.4e38,
                                        op0=ALU.add, op1=ALU.max, accum_out=maxs[:, s % 2, c:c + 1]).then_inc(s_max, 1)
                            for j in range(2):
                                dve.wait_ge(s_max, after_tile(g, s, j, 1))
                                dve.tensor_scalar(nmax[:, s % 2, 2 * j:2 * j + 2], maxs[:, s % 2, 2 * j:2 * j + 2],
                                                  -SCALE, None, ALU.mult).then_inc(s_neg, 1)
                        if (not first or s >= 1) and s - 1 < STEPS:
                            for j in range(2):
                                dve.wait_ge(t_hi, after_head(g, s - 1, j))
                                lo_part(pt_lo[:, j, :], ps_t[j][:, 0:TRI], pt_hi[:, j, :]).then_inc(t_lo, 1)
                        if s == 3:
                            for h in (2, 3):
                                dve.wait_ge(o_hi, HPG * g + h + 1)
                                lo_part(wo_lo[:, h, :], o_scale[:, h, :], wo_hi[:, h, :]).then_inc(o_lo_v, 1)
                        for dg, half, w in pending:
                            unit_rotate(g + dg, half, w)
                        for w in weights_of(s, last):
                            weight_prod(g + 1, w)
                        if s in (6, 7) and not last:
                            for h in (2 * (s - 6), 2 * (s - 6) + 1):
                                out_prod(g + 1, h)
                        if s < STEPS:
                            for j in range(2):
                                dve.wait_ge(s_exp, after_tile(g, s, j, 1))
                                dve.reciprocal(rinv[:, s % 2, 2 * j:2 * j + 2], rsum[:, s % 2, 2 * j:2 * j + 2]).then_inc(s_inv, 1)
                            for j in range(2):
                                dve.wait_ge(s_inv, after_head(g, s, j))
                                for i in range(2):
                                    p = prob[s % 2][:, j, cols[i]]
                                    c = 2 * j + i
                                    dve.tensor_scalar(p, p, rinv[:, s % 2, c:c + 1], None, ALU.mult).then_inc(s_nrm, 1)
                        if out_now:
                            add_out(g, s // 2 - 2, 1)
                        if last and s == STEPS - 2:
                            dve.wait_ge(o_add, after_out(g, 1, 1))
                            stats_dve(dve, 1, 0)
                        if last and s == STEPS:
                            rstd_dve(dve, 1, 0)
                            dve.wait_ge(u_lo, after_unit(g, 1, UNITS - 1))
                            normalise_tiles(dve, 1, 0, rows_2)
                        units = units_of(s, last)
                        for dg, half, w in units[:-1]:
                            unit_rotate(g + dg, half, w)
                        pending = units[-1:]

                groups(dve, body)

            @block.gpsimd
            def _(pool):
                def lo_part(out, full, hi):
                    return pool.tensor_tensor(out, full, f(hi), ALU.subtract)

                def unit_sin(g, half, w):
                    n = unit_slot(half, w)
                    pool.wait_ge(u_swap, 2 * after_unit(g, half, w))
                    pool.tensor_tensor(two(rot[n][:]), two(rot[n][:]), twice(sin_sb), ALU.mult).then_inc(u_sin, 1)

                def unit_lo(g, half, w):
                    hi, lo = u_bufs(half, w)
                    pool.wait_ge(u_hi, after_unit(g, half, w))
                    lo_part(lo, rot[unit_slot(half, w)][:], hi).then_inc(u_lo, 1)

                def weight_lo(g, w):
                    _, prod, hi, lo = w_bufs(w)
                    pool.wait_ge(w_hi, after_weight(g, w))
                    lo_part(lo, prod, hi).then_inc(w_lo, 1)

                for w in range(3):
                    weight_lo(0, w)
                pool.wait_ge(d_const, 3 * 16)
                unit_sin(0, 0, 0)
                weight_lo(0, 3)
                unit_sin(0, 0, 1)
                unit_lo(0, 0, 0)
                weight_lo(0, 4)
                unit_lo(0, 0, 1)
                for w in (2, 3, 4):
                    unit_sin(0, 0, w)
                    unit_lo(0, 0, w)

                def body(g, first, last):
                    pending = [] if first else [(0, 0, UNITS - 1)]
                    for s in range(STEPS):
                        for dg, half, w in pending:
                            unit_lo(g + dg, half, w)
                        pending = units_of(s, last)
                        for w in weights_of(s, last):
                            weight_lo(g + 1, w)
                        if s == 2:
                            for h in (0, 1):
                                pool.wait_ge(o_hi, HPG * g + h + 1)
                                lo_part(wo_lo[:, h, :], o_scale[:, h, :], wo_hi[:, h, :]).then_inc(o_lo_p, 1)
                        for dg, half, w in pending:
                            unit_sin(g + dg, half, w)
                    if last:
                        pool.wait_ge(d_gu, 4 * 16)
                        pool.wait_ge(u_mm, after_unit(g, 1, UNITS - 1))
                        for n in range(2):
                            gate_up_cast(pool, n)

                groups(pool, body)

            @block.tensor
            def _(pe):
                def three(out, a_hi, a_lo, b_hi, b_lo, first, last):
                    pe.matmul(out, a_hi, b_hi, start=first, stop=False)
                    pe.matmul(out, a_hi, b_lo, start=False, stop=False)
                    return pe.matmul(out, a_lo, b_hi, start=False, stop=last)

                def project(g, half, w):
                    _, _, hi, lo = w_bufs(w)
                    n = unit_slot(half, w)
                    pe.wait_ge(w_lo, after_weight(g, w))
                    if earlier(g) or half or w >= 2:
                        pe.wait_ge(u_cos, after_unit(g, half, w) - 2)
                    for k in range(KT):
                        tokens = slice(half * HALF, (half + 1) * HALF)
                        mm = three(ps_unit[n][:], hi[:, k, :], lo[:, k, :], xn_hi[:, k, tokens], xn_lo[:, k, tokens],
                                   k == 0, k == KT - 1)
                    mm.then_inc(u_mm, 1)

                pe.wait_ge(d_id, 16)
                xn_pe(pe, 0, 0, rows_1[0], four_banks)
                pe.wait_ge(ln_lo, TP)
                for w in range(3):
                    project(0, 0, w)
                xn_pe(pe, 0, 1, rows_1[1], four_banks)
                for w in (3, 4):
                    project(0, 0, w)
                for n in range(2 * TT):
                    c, t = n // TT, n % TT
                    if c == 0:
                        pe.wait_ge(ln_lo, t + 1)
                    if n >= 2:
                        pe.wait_ge(v_lo, n - 1)
                    for k in range(KT):
                        if t == 0:
                            pe.wait_ge(vw_lo, KT * c + k + 1)
                        tok, wc = slice(t * P, (t + 1) * P), vw_cols(k)
                        mm = three(ps_s[n % 2][:], xn_hi[:, k, tok], xn_lo[:, k, tok],
                                   vw_hi_sb[c][:, wc], vw_lo_sb[c][:, wc], k == 0, k == KT - 1)
                    mm.then_inc(v_mm, 1)

                def output(g, b, i):
                    pe.wait_ge(pv_lo, after_step(g, 2 * b + 1))
                    if not (isinstance(g, int) and g == 0 and b == 0 and i == 0):
                        pe.wait_ge(o_add, after_out(g, b, i) - 1)
                    gw = g if b >= 0 else g - 1
                    for h in range(HPG):
                        if h == 0:
                            pe.wait_ge(o_lo_p, 2 * gw + 2)
                        if h == 2:
                            pe.wait_ge(o_lo_v, 2 * gw + 2)
                        q = slice(i * P, (i + 1) * P)
                        mm = three(ps_o[:], at_hi[:, b % 2, h, q], at_lo[:, b % 2, h, q], wo_hi[:, h, :], wo_lo[:, h, :],
                                   h == 0, h == HPG - 1)
                    mm.then_inc(o_mm, 1)

                def scores(g, s, first):
                    b = s // 2
                    half, at = b // 2, (b % 2) * SEQ
                    for j in range(2):
                        h = 2 * (s % 2) + j
                        pe.wait_ge(u_lo, after_unit(g, half, 1 + h))
                        if not first or s >= 1:
                            pe.wait_ge(s_max, after_tile(g, s - 1, j, 1))
                        else:
                            pe.wait_ge(v_lo, 2 * TT)
                        for i in range(2):
                            q, kk = slice(at + i * P, at + (i + 1) * P), slice(at, at + (i + 1) * P)
                            mm = three(ps_s[j][:, cols[i]], q_hi[:, h, half, q], q_lo[:, h, half, q],
                                       k_hi[:, half, kk], k_lo[:, half, kk], True, True)
                        mm.then_inc(s_mm, 1)

                def transposes(g, s, first):
                    for j in range(2):
                        pe.wait_ge(s_nrm, after_tile(g, s, j, 1))
                        if not first or s >= 1:
                            pe.wait_ge(t_lo, after_head(g, s - 1, j))
                        for n in range(3):
                            mm = pe.transpose(ps_t[j][:, n * P:(n + 1) * P], prob[s % 2][:, j, n * P:(n + 1) * P], ident[:])
                        mm.then_inc(t_mm, 1)

                def values(g, s, first):
                    b = s // 2
                    pe.wait_ge(d_vin[b], 32 * (g + 1))
                    pe.wait_ge(t_lo, after_head(g, s, 1))
                    if not first or s >= 1:
                        pe.wait_ge(pv_lo, after_step(g, s - 1))
                    for n in range(2):
                        out = ps_pv[:] if n == 0 else two(ps_pv[:])[:, :, P:SEQ]
                        kcols = slice(0, SEQ) if n == 0 else slice(SEQ, TRI)
                        if n == 0:
                            out = two(ps_pv[:])
                        mm = three(out, vg_hi[:, 2 * b + n, :], vg_lo[:, 2 * b + n, :],
                                   pt_hi[:, :, kcols], pt_lo[:, :, kcols], n == 0, n == 1)
                    mm.then_inc(pv_mm, 1)

                def body(g, first, last):
                    for s in range(STEPS + (3 if last else 0)):
                        if s < STEPS:
                            scores(g, s, first)
                        if (not first or s >= 1) and s - 1 < STEPS:
                            if s == 0:
                                transposes(g - 1, STEPS - 1, False)
                            else:
                                transposes(g, s - 1, first)
                        if s % 2 == 0 and (not first or s >= 4):
                            output(g, s // 2 - 2, 1)
                        for dg, half, w in units_of(s, last):
                            project(g + dg, half, w)
                        if (not first or s >= 1) and s - 1 < STEPS:
                            if s == 0:
                                values(g - 1, STEPS - 1, False)
                            else:
                                values(g, s - 1, first)
                        if last and s == STEPS:
                            xn_pe(pe, 1, 0, rows_2, ps_unit)
                            gate_up(pe, 0)
                        if s % 2 == 1 and (not first or s >= 3) and s - 3 < STEPS:
                            output(g, (s - 3) // 2, 0)
                        if last and s == STEPS + 1:
                            gate_up(pe, 1)

                groups(pe, body)

        attn_scope.close()

        wd_16 = sb("wd_16", [P, MT, HID], F16)
        wd_32 = sb("wd_32", [P, MT, HID], F32R)
        h_hi = sb("h_hi", [P, MT, HALF], F32R)
        h_lo = sb("h_lo", [P, MT, HALF], F32R)
        sg = [sb(f"sg{i}", [P, HALF], F32) for i in range(2)]
        hh = [sb(f"hh{i}", [P, HALF], F32) for i in range(2)]

        with nc.Block() as block:

            @block.sync
            def _(sp):
                sp.dma_start(wd_16[:], wd).then_inc(d_wd, 16)
                for t in range(TT):
                    sp.wait_ge(f_add, t + 1)
                    sp.dma_start(out[t], acc[:, t, :]).then_inc(d_out, 16)
                sp.wait_ge(d_out, 16 * TT)

            @block.scalar
            def _(act):
                def hidden_hi(n):
                    act.wait_ge(f_h, n + 1)
                    if n == MT:
                        act.wait_ge(f_dn, TP)
                    act.activation(h_hi[:, n % MT, :], hh[n % 2][:], ACT.Copy).then_inc(f_hi, 1)

                sqrt_act(act, 1, 1)
                for n in range(NHALF * MT):
                    if n == MT:
                        hidden_hi(n - 1)
                    act.wait_ge(f_gu, 2 * n + 1)
                    if n >= 2:
                        act.wait_ge(f_h, n - 1)
                    act.activation(sg[n % 2][:], ps_gate[n % 2][:], ACT.Silu).then_inc(f_sg, 1)
                    if n >= 1 and n != MT:
                        hidden_hi(n - 1)
                    if n == 1:
                        xn_hi_act(act, 1, 1, four_banks)
                hidden_hi(NHALF * MT - 1)

            @block.vector
            def _(dve):
                dve.wait_ge(o_add, TT * NKV)
                stats_dve(dve, 1, 1)
                rstd_dve(dve, 1, 1)
                normalise_tiles(dve, 1, 1, rows_2)

                def hidden(n):
                    dve.wait_ge(f_sg, n + 1)
                    dve.wait_ge(f_gu, 2 * n + 2)
                    if n >= 2:
                        dve.wait_ge(f_lo, n - 1)
                    dve.tensor_tensor(hh[n % 2][:], sg[n % 2][:], ps_up[n % 2][:], ALU.mult).then_inc(f_h, 1)

                def hidden_lo(n):
                    dve.wait_ge(f_hi, n + 1)
                    dve.tensor_tensor(h_lo[:, n % MT, :], hh[n % 2][:], f(h_hi[:, n % MT, :]), ALU.subtract).then_inc(f_lo, 1)

                def down_add(t):
                    dve.wait_ge(f_dn, t + 1)
                    dve.tensor_tensor(acc[:, t, :], acc[:, t, :], ps_dn[t % 2][:], ALU.add).then_inc(f_add, 1)

                for n in range(NHALF * MT):
                    if n == MT:
                        hidden_lo(n - 1)
                        for t in range(TP):
                            down_add(t)
                    hidden(n)
                    if n >= 1 and n != MT:
                        hidden_lo(n - 1)
                    if n == 1:
                        xn_lo_dve(dve, 1, 1, four_banks)
                hidden_lo(NHALF * MT - 1)
                for t in range(TP, TT):
                    down_add(t)

            @block.gpsimd
            def _(pool):
                for n in range(2, NHALF * MT):
                    pool.wait_ge(f_gu, 2 * n - 2)
                    gate_up_cast(pool, n)
                    for m in range(2 * n - 4, min(2 * n - 2, MT)):
                        if m == 0:
                            pool.wait_ge(d_wd, 16)
                        pool.tensor_scalar(wd_32[:, m, :], wd_16[:, m, :], 1.0, 1.0, ALU.mult, ALU.mult).then_inc(f_dcast, 1)

            @block.tensor
            def _(pe):
                for n in range(NHALF * MT):
                    hf = n // MT
                    if n >= 2:
                        gate_up(pe, n)
                    if n == 1:
                        xn_pe(pe, 1, 1, rows_2, four_banks)
                    if n % MT < MT - 1:
                        continue
                    pe.wait_ge(f_dcast, MT)
                    for t in tiles(hf):
                        if t >= 2:
                            pe.wait_ge(f_add, t - 1)
                        for m in range(MT):
                            if t == TP * hf:
                                pe.wait_ge(f_lo, MT * hf + m + 1)
                            for part in (h_hi, h_lo):
                                mm = pe.matmul(ps_dn[t % 2][:], part[:, m, (t % TP) * P:(t % TP + 1) * P], wd_32[:, m, :],
                                               start=(m == 0 and part is h_hi), stop=(m == MT - 1 and part is h_lo))
                        mm.then_inc(f_dn, 1)


def kernel(**inputs):
    import numpy as np
    import concourse.bacc as bacc
    from concourse.bass_utils import run_bass_kernel_spmd

    a = {n.removeprefix("L0_attn_").removeprefix("L0_ffn_"): np.asarray(v) for n, v in inputs.items()}

    def halves(w):
        return w.reshape(w.shape[0], -1, P // 2, 2).swapaxes(2, 3).reshape(w.shape)

    q_c = halves(a["q_codes"]).reshape(KT, P, NKV, HPG, P).transpose(2, 1, 3, 0, 4)
    q_s = halves(a["q_scales"]).reshape(KT, NKV, HPG, P).transpose(1, 2, 0, 3).reshape(NKV, -1)
    k_c = halves(a["k_codes"]).reshape(KT, P, NKV, P).transpose(2, 1, 0, 3)
    k_s = halves(a["k_scales"]).reshape(KT, NKV, P).transpose(1, 0, 2).reshape(NKV, -1)
    v_c = a["v_codes"].reshape(KT, P, 2, HALF).transpose(2, 1, 0, 3).reshape(2, P, -1)
    v_s = a["v_scales"].reshape(KT, 2, HALF).transpose(1, 0, 2).reshape(2, -1)
    o_c = a["o_codes"].reshape(NKV, HPG, P, HID).transpose(0, 2, 1, 3)
    o_s = a["o_scales"].reshape(NKV, -1)

    def ffn(w):
        return w.reshape(2, MH, P, KT, P).transpose(0, 4, 1, 3, 2).reshape(2, P, -1)

    w_d = a["W_down"].reshape(HID, MT, P).transpose(2, 1, 0)

    inv_freq = (1.0 / np.float32(10000.0) ** (np.arange(0, P, 2, dtype=np.float32) / np.float32(P))).astype(np.float32)
    angle = inv_freq[:, None] * np.arange(SEQ, dtype=np.float32)[None, :]
    cos = np.concatenate([np.cos(angle)] * 2).astype(np.float32)
    sin = np.concatenate([-np.sin(angle), np.sin(angle)]).astype(np.float32)
    mask = np.zeros((P, SEQ), np.float32)
    mask[:, P:] = np.where(np.arange(P)[None, :] <= np.arange(P)[:, None], 0.0, MASKED)

    arrays = {
        "x": a["hidden_states"].reshape(TT, P, HID), "qc": q_c, "qs": q_s, "kc": k_c, "ks": k_s, "vc": v_c, "vs": v_s,
        "oc": o_c, "os": o_s, "wg": ffn(a["W_gate"]), "wu": ffn(a["W_up"]), "wd": w_d,
        "rope_cos": cos, "rope_sin": sin, "causal": mask, "eye": np.eye(P, dtype=np.float32),
    }
    arrays = {n: np.ascontiguousarray(v) for n, v in arrays.items()}
    nc = bacc.Bacc("TRN2", target_bir_lowering=False, num_devices=1)
    args = [nc.dram_tensor(n, v.shape, mybir.dt.from_np(v.dtype), kind="ExternalInput").ap() for n, v in arrays.items()]
    y = nc.dram_tensor("y", (TT, P, HID), F32, kind="ExternalOutput").ap()
    layer_kernel(nc, *args, y)
    r = run_bass_kernel_spmd(nc, [arrays], core_ids=[0])
    return r.results[0]["y"].reshape(BATCH, SEQ, HID)
```

```python
from contextlib import ExitStack

import concourse.bass as bass
from concourse import mybir

F32 = mybir.dt.float32
F32R = mybir.dt.float32r
F16 = mybir.dt.float16
I32 = mybir.dt.int32
ALU = mybir.AluOpType
ACT = mybir.ActivationFunctionType

P = 128
BATCH, SEQ, HID = 4, 256, 512
TOK = BATCH * SEQ
TT = TOK // P
KT = HID // P
NH, NKV = 32, 8
HPG = NH // NKV
FFN = 1792
MT = FFN // P
MH = MT // 2
HALF = 512
NHALF = TOK // HALF
STEPS = 2 * BATCH
EX = 2
UNITS = 1 + HPG
LATE_LN = 5
GU_AHEAD = 4
V_EARLY = 2 * TT - 3
TRI = P + SEQ
SCALE = P ** -0.5
EPS = 1e-5
OFFSET = -8.0
MASKED = -3.0e38


def f(ap):
    return ap.bitcast(F32)


def layer_kernel(nc, x, qc, qs, kc, ks, es, vc, vs, oc, os_, wg, wu, wd, rope_cos, rope_sin, causal, eye, out):
    v_hi_d = nc.dram_tensor("v_hi_scratch", (NKV, TT, P, P), F32, kind="Internal").ap()
    v_lo_d = nc.dram_tensor("v_lo_scratch", (NKV, TT, P, P), F32, kind="Internal").ap()

    with ExitStack() as whole:
        def sem(name):
            return whole.enter_context(nc.semaphore(name))

        def sb(name, shape, dt, ctx=whole):
            return ctx.enter_context(nc.sbuf_tensor(name, shape, dt))

        def bank(name):
            return whole.enter_context(nc.psum_tensor(name, [P, HALF], F32))

        ps_unit = [bank(f"ps_unit{i}") for i in range(1 + EX)]
        ps_s = [bank(f"ps_s{i}") for i in range(2)]
        ps_t = [bank(f"ps_t{i}") for i in range(2)]
        ps_po = bank("ps_po")

        acc = sb("acc", [P, TT, HID], F32)
        xn_hi = sb("xn_hi", [P, KT, TOK], F32R)
        xn_lo = sb("xn_lo", [P, KT, TOK], F32R)
        rot = [sb(f"rot{i}", [P, HALF], F32) for i in range(2)]
        tot = [sb(f"tot{i}", [P, HALF], F32) for i in range(2)]
        k_codes = sb("k_codes", [P, KT, P], I32)
        k_scale = sb("k_scale", [P, KT, P], F32)
        wq_hi = sb("wq_hi", [P, HPG, KT, P], F32R)
        ident = sb("ident", [P, P], F32)
        bn = sb("bn", [P, TT, 6], F32)
        mv = sb("mv", [P, TT, 2], F32)
        ln = sb("ln", [P, 6, TT], F32)
        maxs = sb("maxs", [P, 2, 4], F32)
        nmax = sb("nmax", [P, 2, 4], F32)
        rsum = sb("rsum", [P, 2, 4], F32)
        rinv = sb("rinv", [P, 2, 4], F32)

        d_x = [sem(f"d_x{t}") for t in range(TT)]
        d_id, d_const = sem("d_id"), sem("d_const")
        d_vw = [sem(f"d_vw{c}") for c in range(2)]
        d_vout = [sem(f"d_vout{i}") for i in range(4)]
        d_vin = [sem(f"d_vin{b}") for b in range(BATCH)]
        d_kw, d_qw, d_oc, d_os = sem("d_kw"), sem("d_qw"), sem("d_oc"), sem("d_os")
        d_gu, d_wd = sem("d_gu"), sem("d_wd")
        d_out = sem("d_out")
        ln_bn, ln_mv, ln_var, ln_sqrt, ln_chain = sem("ln_bn"), sem("ln_mv"), sem("ln_var"), sem("ln_sqrt"), sem("ln_chain")
        ln_xn, ln_t, ln_hi, ln_lo = sem("ln_xn"), sem("ln_t"), sem("ln_hi"), sem("ln_lo")
        vw_prod, vw_hi, vw_lo = sem("vw_prod"), sem("vw_hi"), sem("vw_lo")
        v_mm, v_hi, v_lo = sem("v_mm"), sem("v_hi"), sem("v_lo")
        w_prod, w_hi, w_lo = sem("w_prod"), sem("w_hi"), sem("w_lo")
        o_prod, o_hi, o_lo_p, o_lo_v = sem("o_prod"), sem("o_hi"), sem("o_lo_p"), sem("o_lo_v")
        d_es, e_copy = sem("d_es"), sem("e_copy")
        u_base, u_acc = sem("u_base"), sem("u_acc")
        u_mm, u_swap, u_cos, u_sin, u_rot, u_hi, u_lo = (sem(n) for n in ("u_mm", "u_swap", "u_cos", "u_sin", "u_rot", "u_hi", "u_lo"))
        s_mm, s_max, s_neg, s_exp, s_inv, s_nrm = (sem(n) for n in ("s_mm", "s_max", "s_neg", "s_exp", "s_inv", "s_nrm"))
        s_seen = sem("s_seen")
        t_mm, t_hi, t_lo = sem("t_mm"), sem("t_hi"), sem("t_lo")
        pv_mm, pv_hi, pv_lo = sem("pv_mm"), sem("pv_hi"), sem("pv_lo")
        o_mm, o_add = sem("o_mm"), sem("o_add")
        f_wcast, f_gu, f_sg, f_h, f_hi, f_lo, f_dcast, f_dn, f_add = (
            sem(n) for n in ("f_wcast", "f_gu", "f_sg", "f_h", "f_hi", "f_lo", "f_dcast", "f_dn", "f_add"))

        def after_head(g, s, j):
            return 2 * STEPS * g + (2 * s + j + 1)

        def after_tile(g, s, j, i):
            return 4 * STEPS * g + (4 * s + 2 * j + i + 1)

        def after_step(g, s):
            return STEPS * g + (s + 1)

        def after_unit(g, half, w):
            return 2 * UNITS * g + (UNITS * half + w + 1)

        def after_weight(g, w):
            return UNITS * g + (w + 1)

        def after_out(g, b, i):
            return TT * g + (2 * b + i + 1)

        def out_bank(s, last):
            return ps_unit[0] if last and 3 <= s <= STEPS else ps_po

        def issued(s, first, last):
            if s < 0:
                return {-1: [(0, 1, 0)], -2: [] if first else [(0, 0, 3), (0, 0, 4)]}[s]
            if s < 3:
                return {0: [(0, 1, 1)], 1: [(0, 1, 2)], 2: [(0, 1, 3), (0, 1, 4)]}[s]
            return [] if last or s >= STEPS else {3: [(1, 0, 0)], 4: [(1, 0, 1)], 5: [(1, 0, 2)], 6: [(1, 0, 3), (1, 0, 4)],
                                                  7: [(1, 1, 0)]}[s]

        def late(s, first, last):
            return issued(s - 1, first, last)[-1:]

        def mid(s, first, last):
            return issued(s, first, last)[:-1] if s >= 0 else []

        def weights_of(s, last):
            return [] if last else {0: [0], 1: [1], 3: [2], 4: [3], 5: [4]}.get(s, [])

        def groups(eng, body):
            body(0, True, False)
            with eng.Fori(1, NKV - 1) as g:
                body(g, False, False)
            body(NKV - 1, False, True)

        def earlier(g):
            return not (isinstance(g, int) and g == 0)

        q_codes = sb("q_codes", [P, HPG, KT, P], I32)
        q_scale = sb("q_scale", [P, HPG, KT, P], F32)
        o_codes = sb("o_codes", [P, HPG, HID], I32)
        o_scale = sb("o_scale", [P, HPG, HID], F32)
        gate_16 = [b.bitcast(F16)[:, 0:MH * KT * P].rearrange("p (m k c) -> p m k c", m=MH, k=KT)
                   for b in (q_codes[:].rearrange("p h k d -> p (h k d)"), q_scale[:].rearrange("p h k d -> p (h k d)"))]
        up_16 = [b.bitcast(F16)[:, 0:MH * KT * P].rearrange("p (m k c) -> p m k c", m=MH, k=KT)
                 for b in (o_codes[:].rearrange("p h n -> p (h n)"), o_scale[:].rearrange("p h n -> p (h n)"))]

        gu_w = [wq_hi[:, 2 * i:2 * i + 2] for i in range(2)]
        k_scale_row = k_scale[:].rearrange("p k d -> p (k d)")
        rows_2 = [rot[0][:], rot[1][:], tot[0][:], tot[1][:]]
        banks_1 = ps_t + ps_s
        banks_2 = [ps_unit[1:] + ps_s, ps_t + [ps_po, ps_unit[2]]]

        TP = TT // 2

        def tiles(part):
            return range(TP * part, TP * part + TP)

        def stats_tile(dve, n, t):
            if n == 0:
                dve.wait_ge(d_x[t], 16)
            dve.bn_stats(bn[:, t, :], acc[:, t, :]).then_inc(ln_bn, 1)

        def stats_finish(dve, n, part):
            for t in tiles(part):
                dve.wait_ge(ln_bn, TT * n + t + 1)
                dve.bn_aggr(mv[:, t, :], bn[:, t, :]).then_inc(ln_mv, 1)
            dve.wait_ge(ln_mv, TT * n + TP * part + TP)
            dve.tensor_scalar(ln[:, 0, TP * part:TP * part + TP], mv[:, TP * part:TP * part + TP, 1], EPS, None,
                              ALU.add).then_inc(ln_var, 1)

        def stats_dve(dve, n, part):
            for t in tiles(part):
                stats_tile(dve, n, t)
            stats_finish(dve, n, part)

        def sqrt_act(act, n, part):
            act.wait_ge(ln_var, 2 * n + part + 1)
            own = slice(TP * part, TP * part + TP)
            act.activation(ln[:, 1, own], ln[:, 0, own], ACT.Sqrt).then_inc(ln_sqrt, 1)

        def rstd_dve(dve, n, part):
            v, root, y, a, b, c = (ln[:, i, TP * part:TP * part + TP] for i in range(6))
            k = 5 * (2 * n + part)
            dve.wait_ge(ln_sqrt, 2 * n + part + 1)
            dve.reciprocal(y, root).then_inc(ln_chain, 1)
            dve.wait_ge(ln_chain, k + 1)
            dve.tensor_tensor(a, y, y, ALU.mult).then_inc(ln_chain, 1)
            dve.wait_ge(ln_chain, k + 2)
            dve.tensor_tensor(b, a, v, ALU.mult).then_inc(ln_chain, 1)
            dve.wait_ge(ln_chain, k + 3)
            dve.tensor_scalar(c, b, -0.5, 1.5, ALU.mult, ALU.add).then_inc(ln_chain, 1)
            dve.wait_ge(ln_chain, k + 4)
            dve.tensor_tensor(a, y, c, ALU.mult).then_inc(ln_chain, 1)
            dve.wait_ge(ln_chain, k + 5)

        def normalise_dve(dve, n, t, rows):
            if t >= len(rows):
                dve.wait_ge(ln_t, TT * n + t - len(rows) + 1)
            dve.tensor_scalar(rows[t % len(rows)], acc[:, t, :], mv[:, t, 0:1], ln[:, 3, t:t + 1],
                              ALU.subtract, ALU.mult).then_inc(ln_xn, 1)

        def normalise_tiles(dve, n, part, rows):
            for t in tiles(part):
                normalise_dve(dve, n, t, rows)

        def xn_lo_dve(dve, n, part, banks):
            for t in tiles(part):
                dve.wait_ge(ln_hi, TT * n + t + 1)
                hi, lo = xn_hi[:, :, t * P:(t + 1) * P], xn_lo[:, :, t * P:(t + 1) * P]
                dve.tensor_tensor(lo, banks[t % len(banks)][:].rearrange("p (k c) -> p k c", k=KT), f(hi),
                                  ALU.subtract).then_inc(ln_lo, 1)

        def xn_hi_tile(act, n, t, banks):
            act.wait_ge(ln_t, TT * n + t + 1)
            act.activation(xn_hi[:, :, t * P:(t + 1) * P],
                           banks[t % len(banks)][:].rearrange("p (k c) -> p k c", k=KT), ACT.Copy).then_inc(ln_hi, 1)

        def xn_hi_act(act, n, part, banks):
            for t in tiles(part):
                xn_hi_tile(act, n, t, banks)

        def xn_pe(pe, n, part, rows, banks):
            for t in tiles(part):
                pe.wait_ge(ln_xn, TT * n + t + 1)
                if t >= len(banks):
                    pe.wait_ge(ln_lo, TT * n + t - len(banks) + 1)
                for k in range(KT):
                    last = pe.transpose(banks[t % len(banks)][:, k * P:(k + 1) * P],
                                        rows[t % len(rows)][:, k * P:(k + 1) * P], ident[:])
                last.then_inc(ln_t, 1)

        ps_gate, ps_up, ps_dn = ps_unit, ps_s, ps_t

        sg, hh = rot, tot

        def silu_gate(act, n):
            act.wait_ge(f_gu, 2 * n + 1)
            if n >= 2:
                act.wait_ge(f_h, n - 1)
            act.activation(sg[n % 2][:], ps_gate[n % 2][:], ACT.Silu).then_inc(f_sg, 1)

        def hidden(dve, n):
            dve.wait_ge(f_sg, n + 1)
            dve.wait_ge(f_gu, 2 * n + 2)
            if n >= 2:
                dve.wait_ge(f_lo, n - 1)
            dve.tensor_tensor(hh[n % 2][:], sg[n % 2][:], ps_up[n % 2][:], ALU.mult).then_inc(f_h, 1)

        def gate_up_cast(pool, n):
            if n >= 2:
                pool.wait_ge(f_gu, 2 * n - 2)
            for a, w16 in enumerate((gate_16, up_16)):
                pool.tensor_scalar(gu_w[n % 2][:, a], w16[n % MT // MH][:, n % MT % MH], 1.0, 1.0,
                                   ALU.mult, ALU.mult).then_inc(f_wcast, 1)

        def gate_up(pe, n):
            half = slice(n // MT * HALF, (n // MT + 1) * HALF)
            for a, banks in enumerate((ps_gate, ps_up)):
                pe.wait_ge(f_wcast, 2 * n + a + 1)
                if n % MT == 0:
                    pe.wait_ge(ln_lo, TT + TP * (n // MT + 1))
                if n >= 2:
                    pe.wait_ge(f_h, n - 1)
                for k in range(KT):
                    for part in (xn_hi, xn_lo):
                        mm = pe.matmul(banks[n % 2][:], gu_w[n % 2][:, a, k, :], part[:, k, half],
                                       start=(k == 0 and part is xn_hi), stop=(k == KT - 1 and part is xn_lo))
                mm.then_inc(f_gu, 1)

        attn_scope = whole.enter_context(ExitStack())

        def sba(name, shape, dt):
            return sb(name, shape, dt, attn_scope)

        wq_lo = sba("wq_lo", [P, HPG, KT - EX, P], F32R)
        wk_hi = sba("wk_hi", [P, KT, P], F32R)
        wk_lo = sba("wk_lo", [P, KT - EX, P], F32R)
        rot_c = [sba(f"rot_c{i}", [P, HALF], F32) for i in range(2)]
        e_next = sba("e_next", [P, UNITS, EX], F32)
        e_scale = sba("e_scale", [P, UNITS, EX], F32)
        wo_hi = sba("wo_hi", [P, HPG, HID], F32R)
        wo_lo = sba("wo_lo", [P, HPG, HID], F32R)
        cos_sb = sba("cos_sb", [P, SEQ], F32)
        sin_sb = sba("sin_sb", [P, SEQ], F32)
        mask = sba("mask", [P, SEQ], F32)
        q_hi = sba("q_hi", [P, HPG, NHALF, HALF], F32R)
        q_lo = sba("q_lo", [P, HPG, NHALF, HALF], F32R)
        k_hi = sba("k_hi", [P, NHALF, HALF], F32R)
        k_lo = sba("k_lo", [P, NHALF, HALF], F32R)
        vg_hi = sba("vg_hi", [P, TT, P], F32R)
        vg_lo = sba("vg_lo", [P, TT, P], F32R)
        prob = [sba(f"prob{i}", [P, 2, TRI], F32) for i in range(2)]
        pt_hi = sba("pt_hi", [P, 2, TRI], F32R)
        pt_lo = sba("pt_lo", [P, 2, TRI], F32R)
        at_hi = sba("at_hi", [P, 2, HPG, SEQ], F32R)
        at_lo = sba("at_lo", [P, 2, HPG, SEQ], F32R)

        vw_codes = [o_codes[:].rearrange("p h n -> p (h n)"), q_codes[:].rearrange("p h k d -> p (h k d)")]
        vw_prods = [o_scale[:].rearrange("p h n -> p (h n)"), q_scale[:].rearrange("p h k d -> p (h k d)")]
        vw_hi_sb = [at_hi[:].rearrange("p b h n -> p (b h n)"), wo_hi[:].rearrange("p h n -> p (h n)")]
        vw_lo_sb = [at_lo[:].rearrange("p b h n -> p (b h n)"), wo_lo[:].rearrange("p h n -> p (h n)")]
        v_out_hi = [q_hi[:, i, 1, :] for i in range(4)]
        v_out_lo = [q_lo[:, i, 1, :] for i in range(4)]
        prob_rows = [p[:].rearrange("p j c -> p (j c)")[:, 0:HID] for p in prob]
        rows_1 = [prob_rows + [rot[0][:], rot[1][:]],
                  prob_rows + [k_codes[:].bitcast(F32).rearrange("p k d -> p (k d)"), k_scale_row]]

        def vw_cols(k):
            return slice(k * HALF, (k + 1) * HALF)

        cols = [slice(0, P), slice(P, TRI)]

        def w_bufs(w):
            if w == 0:
                return k_codes[:], k_scale[:], wk_hi[:], wk_lo[:]
            return q_codes[:, w - 1], q_scale[:, w - 1], wq_hi[:, w - 1], wq_lo[:, w - 1]

        def u_bufs(half, w):
            if w == 0:
                return k_hi[:, half, :], k_lo[:, half, :]
            return q_hi[:, w - 1, half, :], q_lo[:, w - 1, half, :]

        def twice(table):
            return table[:].rearrange("p (a s) -> p a s", a=1).broadcast_to([P, 2, SEQ])

        def two(ap):
            return ap.rearrange("p (a s) -> p a s", a=2)

        def v_bank(n):
            return ps_s[n % 2] if n < V_EARLY else ps_po

        def slot(half, w):
            return (UNITS * half + w) % 2

        with nc.Block() as block:

            @block.sync
            def _(sp):
                def load_x(part):
                    for t in tiles(part):
                        sp.dma_start(acc[:, t, :], x[t]).then_inc(d_x[t], 16)

                def load_e(g):
                    sp.dma_start(e_next[:].rearrange("p w k -> p (w k)"),
                                 es[bass.ds(g, 1)].rearrange("g p n -> (g p) n")).then_inc(d_es, 16)

                def load_kq(g):
                    sp.dma_start(k_codes[:], kc[bass.ds(g, 1)].rearrange("g p k d -> (g p) k d")).then_inc(d_kw, 16)
                    sp.dma_start(k_scale[:, EX:].rearrange("p k d -> p (k d)"),
                                 ks[bass.ds(g, 1)].rearrange("g n -> (g n)").partition_broadcast(P)).then_inc(d_kw, 16)
                    sp.dma_start(q_codes[:], qc[bass.ds(g, 1)].rearrange("g p h k d -> (g p) h k d")).then_inc(d_qw, 16)
                    sp.dma_start(q_scale[:, :, EX:].rearrange("p h k d -> p h (k d)"),
                                 qs[bass.ds(g, 1)].rearrange("g h n -> (g h) n").partition_broadcast(P)).then_inc(d_qw, 16)

                def load_oc(g):
                    sp.dma_start(o_codes[:], oc[bass.ds(g, 1)].rearrange("g p h n -> (g p) h n")).then_inc(d_oc, 16)

                def load_os(g):
                    sp.dma_start(o_scale[:].rearrange("p h n -> p (h n)"),
                                 os_[bass.ds(g, 1)].rearrange("g n -> (g n)").partition_broadcast(P)).then_inc(d_os, 16)

                def load_v(g, b):
                    for dst, src in ((vg_hi, v_hi_d), (vg_lo, v_lo_d)):
                        sp.dma_start(f(dst[:, 2 * b:2 * b + 2, :]),
                                     src[bass.ds(g, 1), 2 * b:2 * b + 2].rearrange("g t p d -> p (g t) d")).then_inc(d_vin[b], 16)

                def load_vw(c):
                    sp.dma_start(vw_codes[c], vc[c]).then_inc(d_vw[c], 16)
                    sp.dma_start(vw_prods[c], vs[c].partition_broadcast(P)).then_inc(d_vw[c], 16)

                load_x(0)
                sp.dma_start(ident[:], eye).then_inc(d_id, 16)
                load_kq(0)
                load_e(0)
                load_x(1)
                for dst, src in ((cos_sb, rope_cos), (sin_sb, rope_sin), (mask, causal)):
                    sp.dma_start(dst[:], src).then_inc(d_const, 16)
                load_vw(0)
                sp.wait_ge(w_lo, UNITS)
                load_vw(1)
                sp.wait_ge(vw_lo, KT)
                load_oc(0)
                load_os(0)
                for n in range(2 * TT):
                    c, t = n // TT, n % TT
                    if n == V_EARLY:
                        load_kq(1)
                        sp.wait_ge(e_copy, 1)
                        load_e(1)
                    if n == TT:
                        for i in range(4):
                            sp.wait_ge(d_vout[i], 32 * 2)
                        for b in range(BATCH):
                            load_v(0, b)
                    sp.wait_ge(v_lo, n + 1)
                    for src, dst in ((v_out_hi, v_hi_d), (v_out_lo, v_lo_d)):
                        sp.dma_start(dst[4 * c:4 * c + 4, t].rearrange("g p d -> p g d"),
                                     f(src[n % 4]).rearrange("p (g d) -> p g d", g=4)).then_inc(d_vout[n % 4], 16)
                for i in range(4):
                    sp.wait_ge(d_vout[i], 32 * 4)

                def body(g, first, last):
                    if not first and not last:
                        sp.wait_ge(w_lo, after_weight(g, UNITS - 1))
                        load_kq(g + 1)
                        sp.wait_ge(e_copy, g + 1)
                        load_e(g + 1)
                    if not last:
                        sp.wait_ge(o_prod, HPG * g + HPG)
                        load_oc(g + 1)
                    if not first:
                        sp.wait_ge(pv_mm, after_step(g, 0) - 1)
                        load_v(g, BATCH - 1)
                    if not last:
                        sp.wait_ge(o_lo_p, 2 * g + 2)
                        sp.wait_ge(o_lo_v, 2 * g + 2)
                        load_os(g + 1)
                        for b in range(BATCH - 1):
                            sp.wait_ge(pv_mm, after_step(g, 2 * b + 1))
                            load_v(g + 1, b)

                groups(sp, body)
                sp.wait_ge(w_lo, after_weight(NKV - 1, UNITS - 1))
                for a in range(2):
                    sp.dma_start(gate_16[a].rearrange("p m k c -> p (m k c)"), wg[a]).then_inc(d_gu, 16)
                sp.wait_ge(o_lo_p, 2 * NKV)
                sp.wait_ge(o_lo_v, 2 * NKV)
                for a in range(2):
                    sp.dma_start(up_16[a].rearrange("p m k c -> p (m k c)"), wu[a]).then_inc(d_gu, 16)

            @block.scalar
            def _(act):
                def copy(out, in_):
                    return act.activation(out, in_, ACT.Copy)

                def unit_base(g, half, w):
                    act.wait_ge(u_mm, after_unit(g, half, w))
                    if earlier(g) or half or w >= 2:
                        act.wait_ge(u_swap, 2 * (after_unit(g, half, w) - 2))
                        act.wait_ge(u_cos, after_unit(g, half, w) - 2)
                    copy(tot[slot(half, w)][:], ps_unit[0][:]).then_inc(u_base, 1)

                def unit_swap(g, half, w):
                    n = slot(half, w)
                    act.wait_ge(u_acc, EX * after_unit(g, half, w))
                    if earlier(g) or half or w >= 2:
                        act.wait_ge(u_lo, after_unit(g, half, w) - 2)
                    copy(rot[n][0:64, :], tot[n][64:128, :]).then_inc(u_swap, 1)
                    copy(rot[n][64:128, :], tot[n][0:64, :]).then_inc(u_swap, 1)

                def unit_hi(g, half, w):
                    hi, _ = u_bufs(half, w)
                    act.wait_ge(u_rot, after_unit(g, half, w))
                    if earlier(g):
                        act.wait_ge(s_mm, after_head(g - 1, 4 * half + 3, 1))
                    elif half and w:
                        act.wait_ge(d_vout[w - 1], 32 * 4)
                    copy(hi, rot[slot(half, w)][:]).then_inc(u_hi, 1)

                def weight_hi(g, w):
                    codes, prod, hi, _ = w_bufs(w)
                    act.wait_ge(d_kw if w == 0 else d_qw, 32 * (g + 1))
                    if earlier(g):
                        act.wait_ge(u_mm, after_unit(g - 1, 1, w))
                    act.activation(hi[:, 0:EX], codes[:, 0:EX], ACT.Copy, bias=OFFSET).then_inc(w_hi, 1)
                    act.wait_ge(w_prod, after_weight(g, w))
                    copy(hi[:, EX:], prod[:, EX:]).then_inc(w_hi, 1)

                def out_weights_hi(heads):
                    for h in heads:
                        copy(wo_hi[:, h, :], o_scale[:, h, :]).then_inc(o_hi, 1)

                def v_part_hi(n):
                    act.wait_ge(v_mm, n + 1)
                    if n >= 4:
                        act.wait_ge(d_vout[n % 4], 32 * (n // 4))
                    copy(v_out_hi[n % 4], v_bank(n)[:]).then_inc(v_hi, 1)

                def v_weights_hi(c, k):
                    act.wait_ge(vw_prod, KT * c + k + 1)
                    copy(vw_hi_sb[c][:, vw_cols(k)], vw_prods[c][:, vw_cols(k)]).then_inc(vw_hi, 1)

                sqrt_act(act, 0, 0)
                xn_hi_tile(act, 0, 0, banks_1)
                weight_hi(0, 0)
                for t in range(1, TP):
                    xn_hi_tile(act, 0, t, banks_1)
                for w in (1, 2):
                    weight_hi(0, w)
                sqrt_act(act, 0, 1)
                unit_base(0, 0, 0)
                weight_hi(0, 3)
                xn_hi_act(act, 0, 1, banks_1)
                unit_swap(0, 0, 0)
                v_weights_hi(0, 0)
                unit_base(0, 0, 1)
                v_weights_hi(0, 1)
                v_weights_hi(0, 2)
                v_weights_hi(0, 3)
                unit_swap(0, 0, 1)
                weight_hi(0, 4)
                unit_hi(0, 0, 0)
                unit_base(0, 0, 2)
                unit_swap(0, 0, 2)
                unit_hi(0, 0, 1)
                for n in range(V_EARLY):
                    v_part_hi(n)
                    if n < 2:
                        unit_base(0, 0, n + 3)
                        unit_swap(0, 0, n + 3)
                        unit_hi(0, 0, n + 2)
                    if n == 2:
                        unit_hi(0, 0, UNITS - 1)
                    if 3 <= n < 3 + KT:
                        v_weights_hi(1, n - 3)
                unit_base(0, 1, 0)

                def body(g, first, last):
                    for s in range(STEPS + (3 if last else 0)):
                        if (not first or s >= 2) and s - 2 < STEPS:
                            act.wait_ge(pv_mm, after_step(g, s - 2))
                            if not first or s >= 6:
                                act.wait_ge(o_mm, after_out(g, (s - 2) // 2 - 2, 1))
                            copy(at_hi[:, ((s - 2) // 2) % 2, 2 * (s % 2):2 * (s % 2) + 2, :], two(ps_po[:])).then_inc(pv_hi, 1)
                        if last and s == STEPS + 1:
                            xn_hi_act(act, 1, 0, banks_2[0])
                        for dg, half, w in late(s, first, last):
                            unit_swap(g + dg, half, w)
                        if (not first or s >= 1) and s - 1 < STEPS:
                            for j in range(2):
                                act.wait_ge(t_mm, after_head(g, s - 1, j))
                                if not first or s >= 2:
                                    act.wait_ge(pv_mm, after_step(g, s - 2))
                                copy(pt_hi[:, j, :], ps_t[j][:, 0:TRI]).then_inc(t_hi, 1)
                        if s < STEPS:
                            for j in range(2):
                                act.wait_ge(s_neg, after_head(g, s, j))
                                for i in range(2):
                                    p = prob[s % 2][:, j, cols[i]]
                                    c = 2 * j + i
                                    act.activation(p, p, ACT.Exp, bias=nmax[:, s % 2, c:c + 1], scale=SCALE,
                                                   accum_out=rsum[:, s % 2, c:c + 1]).then_inc(s_exp, 1)
                                if j == 0:
                                    for dg, half, w in mid(s, first, last):
                                        unit_base(g + dg, half, w)
                        if first and s < 3:
                            v_part_hi(V_EARLY + s)
                        if s == 2:
                            act.wait_ge(o_prod, HPG * g + HPG)
                            if not first:
                                act.wait_ge(o_mm, after_out(g - 1, BATCH - 1, 1))
                            else:
                                act.wait_ge(v_mm, 2 * TT)
                            out_weights_hi((0, 1))
                        for dg, half, w in mid(s - 1, first, last) + late(s, first, last):
                            unit_hi(g + dg, half, w)
                        for dg, half, w in mid(s, first, last):
                            unit_swap(g + dg, half, w)
                        for dg, half, w in issued(s, first, last)[-1:]:
                            unit_base(g + dg, half, w)
                        if s == 2:
                            out_weights_hi((2, 3))
                        if last and s == STEPS - 1:
                            sqrt_act(act, 1, 0)
                        if last and s == STEPS + 1:
                            silu_gate(act, 0)
                        for w in weights_of(s, last):
                            weight_hi(g + 1, w)

                groups(act, body)

            @block.vector
            def _(dve):
                def lo_part(out, full, hi):
                    return dve.tensor_tensor(out, full, f(hi), ALU.subtract)

                def product(codes, scale):
                    return dve.scalar_tensor_tensor(out=scale, in0=codes, scalar=OFFSET, in1=scale, op0=ALU.add, op1=ALU.mult)

                def weight_prod(g, w):
                    codes, scale, _, _ = w_bufs(w)
                    dve.wait_ge(d_kw if w == 0 else d_qw, 32 * (g + 1))
                    product(codes[:, EX:], scale[:, EX:]).then_inc(w_prod, 1)

                def out_prod(g, h):
                    dve.wait_ge(d_oc, 16 * (g + 1))
                    dve.wait_ge(d_os, 16 * (g + 1))
                    product(o_codes[:, h, :], o_scale[:, h, :]).then_inc(o_prod, 1)

                def next_scales(g):
                    dve.wait_ge(d_es, 16 * (g + 1))
                    if earlier(g):
                        dve.wait_ge(u_acc, EX * after_unit(g - 1, 1, UNITS - 1))
                    dve.tensor_copy(e_scale[:], e_next[:]).then_inc(e_copy, 1)

                def out_weights_lo(g, h):
                    dve.wait_ge(o_hi, HPG * g + h + 1)
                    lo_part(wo_lo[:, h, :], o_scale[:, h, :], wo_hi[:, h, :]).then_inc(o_lo_v, 1)

                def unit_gather(g, half, w):
                    n, done = slot(half, w), EX * (after_unit(g, half, w) - 1)
                    if half == 0 and w == 0:
                        dve.wait_ge(e_copy, g + 1)
                    dve.wait_ge(u_base, after_unit(g, half, w))
                    for k in range(EX):
                        if k:
                            dve.wait_ge(u_acc, done + k)
                        dve.scalar_tensor_tensor(out=tot[n][:], in0=ps_unit[1 + k][:], scalar=e_scale[:, w, k:k + 1],
                                                 in1=tot[n][:],
                                                 op0=ALU.mult, op1=ALU.add).then_inc(u_acc, 1)

                def unit_add(g, half, w):
                    n = slot(half, w)
                    dve.wait_ge(u_cos, after_unit(g, half, w))
                    dve.wait_ge(u_sin, after_unit(g, half, w))
                    dve.tensor_tensor(rot[n][:], rot_c[n][:], rot[n][:], ALU.add).then_inc(u_rot, 1)

                def v_part_lo(n):
                    dve.wait_ge(v_hi, n + 1)
                    lo_part(v_out_lo[n % 4], v_bank(n)[:], v_out_hi[n % 4]).then_inc(v_lo, 1)

                def v_weights(c, k):
                    dve.wait_ge(d_vw[c], 32)
                    product(vw_codes[c][:, vw_cols(k)], vw_prods[c][:, vw_cols(k)]).then_inc(vw_prod, 1)

                def v_weights_lo(c, k):
                    dve.wait_ge(vw_hi, KT * c + k + 1)
                    lo_part(vw_lo_sb[c][:, vw_cols(k)], vw_prods[c][:, vw_cols(k)], vw_hi_sb[c][:, vw_cols(k)]).then_inc(vw_lo, 1)

                stats_dve(dve, 0, 0)
                rstd_dve(dve, 0, 0)
                normalise_tiles(dve, 0, 0, rows_1[0])
                weight_prod(0, 0)
                xn_lo_dve(dve, 0, 0, banks_1)
                for w in (1, 2, 3):
                    weight_prod(0, w)
                next_scales(0)
                stats_dve(dve, 0, 1)
                rstd_dve(dve, 0, 1)
                dve.wait_ge(w_lo, 1)
                normalise_tiles(dve, 0, 1, rows_1[1])
                unit_gather(0, 0, 0)
                for k in range(KT):
                    v_weights(0, k)
                unit_gather(0, 0, 1)
                xn_lo_dve(dve, 0, 1, banks_1)
                weight_prod(0, 4)
                for k in range(KT):
                    v_weights_lo(0, k)
                unit_add(0, 0, 0)
                unit_gather(0, 0, 2)
                unit_add(0, 0, 1)
                for n in range(V_EARLY):
                    v_part_lo(n)
                    if n < 2:
                        unit_gather(0, 0, n + 3)
                        unit_add(0, 0, n + 2)
                    if n == 2:
                        unit_add(0, 0, UNITS - 1)
                    if 3 <= n < 3 + KT:
                        v_weights(1, n - 3)
                    if 4 <= n < 4 + KT:
                        v_weights_lo(1, n - 4)
                    if TT <= n < TT + HPG:
                        out_prod(0, n - TT)

                def add_out(g, s, last):
                    dve.wait_ge(o_mm, TT * g + (s - 2))
                    tile = acc[:, (s - 3) % TT, :]
                    dve.tensor_tensor(tile, tile, out_bank(s, last)[:], ALU.add).then_inc(o_add, 1)

                def body(g, first, last):
                    for s in range(STEPS + (3 if last else 0)):
                        if s == 4 and not last:
                            next_scales(g + 1)
                        for dg, half, w in late(s, first, last):
                            unit_gather(g + dg, half, w)
                        if (not first or s >= 2) and s - 2 < STEPS:
                            dve.wait_ge(pv_hi, after_step(g, s - 2))
                            at = ((s - 2) // 2) % 2, slice(2 * (s % 2), 2 * (s % 2) + 2)
                            lo_part(at_lo[:, at[0], at[1], :], two(ps_po[:]), at_hi[:, at[0], at[1], :]).then_inc(pv_lo, 1)
                        if last and s == STEPS + 1:
                            xn_lo_dve(dve, 1, 0, banks_2[0])
                        if s < STEPS:
                            for j in range(2):
                                if not first or s >= 2:
                                    dve.wait_ge(t_mm, after_head(g, s - 2, j))
                                dve.wait_ge(s_mm, after_head(g, s, j))
                                dve.sem_inc(s_seen, 1)
                                for i in range(2):
                                    c = 2 * j + i
                                    dve.tensor_tensor_reduce(
                                        out=prob[s % 2][:, j, cols[i]], in0=ps_s[j][:, cols[i]],
                                        in1=mask[:, P:SEQ] if i == 0 else mask[:], scale=1.0, scalar=-3.4e38,
                                        op0=ALU.add, op1=ALU.max, accum_out=maxs[:, s % 2, c:c + 1]).then_inc(s_max, 1)
                            for j in range(2):
                                dve.wait_ge(s_max, after_tile(g, s, j, 1))
                                dve.tensor_scalar(nmax[:, s % 2, 2 * j:2 * j + 2], maxs[:, s % 2, 2 * j:2 * j + 2],
                                                  -SCALE, None, ALU.mult).then_inc(s_neg, 1)
                        if s == 3:
                            out_weights_lo(g, 3)
                        if (not first or s >= 1) and s - 1 < STEPS:
                            for j in range(2):
                                dve.wait_ge(t_hi, after_head(g, s - 1, j))
                                lo_part(pt_lo[:, j, :], ps_t[j][:, 0:TRI], pt_hi[:, j, :]).then_inc(t_lo, 1)
                        for w in weights_of(s, last):
                            weight_prod(g + 1, w)
                        if s in (0, 1) and not first:
                            out_prod(g, s + 2)
                        if s in (5, 6) and not last:
                            out_prod(g + 1, s - 5)
                        for dg, half, w in mid(s, first, last):
                            unit_gather(g + dg, half, w)
                        if last and s == STEPS:
                            rstd_dve(dve, 1, 0)
                            dve.wait_ge(u_lo, after_unit(g, 1, UNITS - 1))
                            normalise_tiles(dve, 1, 0, rows_2)
                        if not first or s >= 3:
                            add_out(g, s, last)
                        else:
                            v_part_lo(V_EARLY + s)
                        for dg, half, w in mid(s - 1, first, last) + late(s, first, last):
                            unit_add(g + dg, half, w)
                        if s < STEPS:
                            for j in range(2):
                                dve.wait_ge(s_exp, after_tile(g, s, j, 1))
                                dve.reciprocal(rinv[:, s % 2, 2 * j:2 * j + 2], rsum[:, s % 2, 2 * j:2 * j + 2]).then_inc(s_inv, 1)
                            for j in range(2):
                                dve.wait_ge(s_inv, after_head(g, s, j))
                                for i in range(2):
                                    p = prob[s % 2][:, j, cols[i]]
                                    c = 2 * j + i
                                    dve.tensor_scalar(p, p, rinv[:, s % 2, c:c + 1], None, ALU.mult).then_inc(s_nrm, 1)
                        if s == 2:
                            out_weights_lo(g, 0)
                        if last and 4 <= s < STEPS:
                            dve.wait_ge(o_add, TT * g + (s - 3))
                            stats_tile(dve, 1, s - 4)
                        if last and s == STEPS - 1:
                            stats_finish(dve, 1, 0)
                        if last and s == STEPS + 2:
                            hidden(dve, 0)

                groups(dve, body)

            @block.gpsimd
            def _(pool):
                def lo_part(out, full, hi):
                    return pool.tensor_tensor(out, full, f(hi), ALU.subtract)

                def unit_cos_sin(g, half, w):
                    n = slot(half, w)
                    pool.wait_ge(u_acc, EX * after_unit(g, half, w))
                    if earlier(g) or half or w >= 2:
                        pool.wait_ge(u_rot, after_unit(g, half, w) - 2)
                    pool.tensor_tensor(two(rot_c[n][:]), two(tot[n][:]), twice(cos_sb), ALU.mult).then_inc(u_cos, 1)
                    pool.wait_ge(u_swap, 2 * after_unit(g, half, w))
                    pool.tensor_tensor(two(rot[n][:]), two(rot[n][:]), twice(sin_sb), ALU.mult).then_inc(u_sin, 1)

                def unit_lo(g, half, w):
                    hi, lo = u_bufs(half, w)
                    pool.wait_ge(u_hi, after_unit(g, half, w))
                    lo_part(lo, rot[slot(half, w)][:], hi).then_inc(u_lo, 1)

                def out_weights_lo(g, h):
                    pool.wait_ge(o_hi, HPG * g + h + 1)
                    lo_part(wo_lo[:, h, :], o_scale[:, h, :], wo_hi[:, h, :]).then_inc(o_lo_p, 1)

                def weight_lo(g, w):
                    _, prod, hi, lo = w_bufs(w)
                    pool.wait_ge(w_hi, 2 * after_weight(g, w))
                    lo_part(lo, prod[:, EX:], hi[:, EX:]).then_inc(w_lo, 1)

                for w in range(3):
                    weight_lo(0, w)
                pool.wait_ge(d_const, 3 * 16)
                unit_cos_sin(0, 0, 0)
                weight_lo(0, 3)
                weight_lo(0, 4)
                for w in range(1, UNITS):
                    unit_cos_sin(0, 0, w)
                    unit_lo(0, 0, w - 1)
                unit_lo(0, 0, UNITS - 1)

                def body(g, first, last):
                    for s in range(STEPS):
                        for dg, half, w in late(s, first, last):
                            unit_cos_sin(g + dg, half, w)
                        if s == 2:
                            out_weights_lo(g, 1)
                        for dg, half, w in mid(s - 1, first, last) + late(s, first, last):
                            unit_lo(g + dg, half, w)
                        for w in weights_of(s, last):
                            weight_lo(g + 1, w)
                        for dg, half, w in mid(s, first, last):
                            unit_cos_sin(g + dg, half, w)
                        if s == 2:
                            out_weights_lo(g, 2)
                    if last:
                        pool.wait_ge(d_gu, 4 * 16)
                        pool.wait_ge(u_mm, after_unit(g, 1, UNITS - 1))
                        for n in range(GU_AHEAD):
                            gate_up_cast(pool, n)

                groups(pool, body)

            @block.tensor
            def _(pe):
                def three(out, a_hi, a_lo, b_hi, b_lo, first, last):
                    pe.matmul(out, a_hi, b_hi, start=first, stop=False)
                    pe.matmul(out, a_hi, b_lo, start=False, stop=False)
                    return pe.matmul(out, a_lo, b_hi, start=False, stop=last)

                def project_codes(g, half, w):
                    _, _, hi, _ = w_bufs(w)
                    tokens = slice(half * HALF, (half + 1) * HALF)
                    pe.wait_ge(w_lo, after_weight(g, w))
                    for k in range(EX):
                        if earlier(g) or half or w:
                            pe.wait_ge(u_acc, EX * (after_unit(g, half, w) - 2) + k + 1)
                        pe.matmul(ps_unit[1 + k][:], hi[:, k, :], xn_hi[:, k, tokens], start=True, stop=False)
                        pe.matmul(ps_unit[1 + k][:], hi[:, k, :], xn_lo[:, k, tokens], start=False, stop=True)

                def project_products(g, half, w):
                    _, _, hi, lo = w_bufs(w)
                    tokens = slice(half * HALF, (half + 1) * HALF)
                    if earlier(g) or half or w:
                        pe.wait_ge(u_base, after_unit(g, half, w) - 1)
                    for k in range(EX, KT):
                        mm = three(ps_unit[0][:], hi[:, k, :], lo[:, k - EX, :], xn_hi[:, k, tokens], xn_lo[:, k, tokens],
                                   k == EX, k == KT - 1)
                    mm.then_inc(u_mm, 1)

                def project(g, half, w):
                    project_codes(g, half, w)
                    project_products(g, half, w)

                def v_unit(n):
                    c, t = n // TT, n % TT
                    for k in range(KT):
                        if t == 0:
                            pe.wait_ge(vw_lo, KT * c + k + 1)
                        tok, wc = slice(t * P, (t + 1) * P), vw_cols(k)
                        mm = three(v_bank(n)[:], xn_hi[:, k, tok], xn_lo[:, k, tok],
                                   vw_hi_sb[c][:, wc], vw_lo_sb[c][:, wc], k == 0, k == KT - 1)
                    mm.then_inc(v_mm, 1)

                pe.wait_ge(d_id, 16)
                xn_pe(pe, 0, 0, rows_1[0], banks_1)
                pe.wait_ge(ln_lo, TP)
                project(0, 0, 0)
                xn_pe(pe, 0, 1, rows_1[1], banks_1)
                project(0, 0, 1)
                project(0, 0, 2)
                pe.wait_ge(ln_lo, TT)
                for n in range(V_EARLY):
                    if n >= 2:
                        pe.wait_ge(v_lo, n - 1)
                    v_unit(n)
                    if n < 2:
                        project(0, 0, n + 3)
                project(0, 1, 0)

                def output(g, s, last):
                    b, i = (s - 3) // 2, (s - 3) % 2
                    if i == 0 or out_bank(s, last) is ps_po:
                        pe.wait_ge(pv_lo, after_step(g, min(s - 2, STEPS - 1)))
                    if last and s == 3:
                        pe.wait_ge(u_base, after_unit(g, 1, UNITS - 1))
                    if last and (3 < s <= STEPS or s > STEPS + 1):
                        pe.wait_ge(o_add, TT * g + (s - 3))
                    gw = g if b >= 0 else g - 1
                    for h in range(HPG):
                        pe.wait_ge(o_lo_v if h in (0, 3) else o_lo_p, 2 * gw + 1 + h // 2)
                        q = slice(i * P, (i + 1) * P)
                        mm = three(out_bank(s, last)[:], at_hi[:, b % 2, h, q], at_lo[:, b % 2, h, q], wo_hi[:, h, :], wo_lo[:, h, :],
                                   h == 0, h == HPG - 1)
                    mm.then_inc(o_mm, 1)

                def scores(g, s, first):
                    b = s // 2
                    half, at = b // 2, (b % 2) * SEQ
                    for j in range(2):
                        h = 2 * (s % 2) + j
                        pe.wait_ge(u_lo, after_unit(g, half, 1 + h))
                        if not first or s >= 1:
                            pe.wait_ge(s_max, after_tile(g, s - 1, j, 1))
                        else:
                            pe.wait_ge(v_lo, V_EARLY)
                        for i in range(2):
                            q, kk = slice(at + i * P, at + (i + 1) * P), slice(at, at + (i + 1) * P)
                            mm = three(ps_s[j][:, cols[i]], q_hi[:, h, half, q], q_lo[:, h, half, q],
                                       k_hi[:, half, kk], k_lo[:, half, kk], True, True)
                        mm.then_inc(s_mm, 1)

                def transposes(g, s, first):
                    for j in range(2):
                        pe.wait_ge(s_nrm, after_tile(g, s, j, 1))
                        if not first or s >= 1:
                            pe.wait_ge(t_lo, after_head(g, s - 1, j))
                        for n in range(3):
                            mm = pe.transpose(ps_t[j][:, n * P:(n + 1) * P], prob[s % 2][:, j, n * P:(n + 1) * P], ident[:])
                        mm.then_inc(t_mm, 1)

                def values(g, s, first, last):
                    b = s // 2
                    pe.wait_ge(d_vin[b], 32 * (g + 1))
                    pe.wait_ge(t_lo, after_head(g, s, 1))
                    if last and s >= 2:
                        pe.wait_ge(pv_lo, after_step(g, s - 1))
                    elif not first or s >= 2:
                        pe.wait_ge(o_add, TT * g + (s - 1))
                    else:
                        pe.wait_ge(v_lo, V_EARLY + s + 2)
                    for n in range(2):
                        out = two(ps_po[:]) if n == 0 else two(ps_po[:])[:, :, P:SEQ]
                        kcols = slice(0, SEQ) if n == 0 else slice(SEQ, TRI)
                        mm = three(out, vg_hi[:, 2 * b + n, :], vg_lo[:, 2 * b + n, :],
                                   pt_hi[:, :, kcols], pt_lo[:, :, kcols], n == 0, n == 1)
                    mm.then_inc(pv_mm, 1)

                def body(g, first, last):
                    for s in range(STEPS + (3 if last else 0)):
                        if s < STEPS:
                            scores(g, s, first)
                        if (not first or s >= 1) and s - 1 < STEPS:
                            if s == 0:
                                transposes(g - 1, STEPS - 1, False)
                            else:
                                transposes(g, s - 1, first)
                        for dg, half, w in mid(s, first, last):
                            project(g + dg, half, w)
                        units = issued(s, first, last)[-1:]
                        for dg, half, w in units if not mid(s, first, last) else []:
                            project_codes(g + dg, half, w)
                        if not first or s >= 3:
                            output(g, s, last)
                        else:
                            if s == 1:
                                pe.wait_ge(v_lo, V_EARLY + s)
                            if s == 2:
                                pe.wait_ge(pv_lo, after_step(g, 0))
                            v_unit(V_EARLY + s)
                        if last and s > STEPS:
                            gate_up(pe, s - STEPS - 1)
                        for dg, half, w in units:
                            if mid(s, first, last):
                                project_codes(g + dg, half, w)
                            project_products(g + dg, half, w)
                        if (not first or s >= 1) and s - 1 < STEPS:
                            if s == 0:
                                values(g - 1, STEPS - 1, False, False)
                            else:
                                values(g, s - 1, first, last)
                        if last and s == STEPS:
                            xn_pe(pe, 1, 0, rows_2, banks_2[0])

                groups(pe, body)

        attn_scope.close()

        wd_16 = sb("wd_16", [P, MT, HID], F16)
        wd_32 = sb("wd_32", [P, MT, HID], F32R)
        h_hi = sb("h_hi", [P, MT, HALF], F32R)
        h_lo = sb("h_lo", [P, MT, HALF], F32R)
        rows_late = [sb(f"row_late{i}", [P, HALF], F32)[:] for i in range(TP)]

        with nc.Block() as block:

            @block.sync
            def _(sp):
                sp.dma_start(wd_16[:], wd).then_inc(d_wd, 16)
                for t in range(TT):
                    sp.wait_ge(f_add, t + 1)
                    sp.dma_start(out[t], acc[:, t, :]).then_inc(d_out, 16)
                sp.wait_ge(d_out, 16 * TT)

            @block.scalar
            def _(act):
                def hidden_hi(n):
                    act.wait_ge(f_h, n + 1)
                    if n == MT:
                        act.wait_ge(f_dn, TP)
                    act.activation(h_hi[:, n % MT, :], hh[n % 2][:], ACT.Copy).then_inc(f_hi, 1)

                for n in range(NHALF * MT):
                    if n == MT:
                        hidden_hi(n - 1)
                    if n >= 1:
                        silu_gate(act, n)
                    if n >= 1 and n != MT:
                        hidden_hi(n - 1)
                    if n == LATE_LN - 3:
                        sqrt_act(act, 1, 1)
                    if n == LATE_LN:
                        xn_hi_act(act, 1, 1, banks_2[1])
                hidden_hi(NHALF * MT - 1)

            @block.vector
            def _(dve):

                def hidden_lo(n):
                    dve.wait_ge(f_hi, n + 1)
                    dve.tensor_tensor(h_lo[:, n % MT, :], hh[n % 2][:], f(h_hi[:, n % MT, :]), ALU.subtract).then_inc(f_lo, 1)

                def down_add(t):
                    dve.wait_ge(f_dn, t + 1)
                    dve.tensor_tensor(acc[:, t, :], acc[:, t, :], ps_dn[t % 2][:], ALU.add).then_inc(f_add, 1)

                for n in range(NHALF * MT):
                    if n == MT:
                        hidden_lo(n - 1)
                        for t in range(TP):
                            down_add(t)
                    if n >= 1:
                        hidden(dve, n)
                    if n >= 1 and n != MT:
                        hidden_lo(n - 1)
                    if n == LATE_LN - 3:
                        dve.wait_ge(o_add, TT * NKV)
                        stats_dve(dve, 1, 1)
                    if n == LATE_LN - 2:
                        rstd_dve(dve, 1, 1)
                        normalise_tiles(dve, 1, 1, rows_late)
                    if n == LATE_LN:
                        xn_lo_dve(dve, 1, 1, banks_2[1])
                hidden_lo(NHALF * MT - 1)
                for t in range(TP, TT):
                    down_add(t)

            @block.gpsimd
            def _(pool):
                for n in range(GU_AHEAD, NHALF * MT):
                    gate_up_cast(pool, n)
                    for m in range(max(2 * n - 8, 0), min(2 * n - 6, MT)):
                        if m == 0:
                            pool.wait_ge(d_wd, 16)
                        pool.tensor_scalar(wd_32[:, m, :], wd_16[:, m, :], 1.0, 1.0, ALU.mult, ALU.mult).then_inc(f_dcast, 1)

            @block.tensor
            def _(pe):
                for n in range(NHALF * MT):
                    hf = n // MT
                    if n >= 2:
                        gate_up(pe, n)
                    if n == LATE_LN:
                        xn_pe(pe, 1, 1, rows_late, banks_2[1])
                    if n % MT < MT - 1:
                        continue
                    pe.wait_ge(f_dcast, MT)
                    for t in tiles(hf):
                        if t >= 2:
                            pe.wait_ge(f_add, t - 1)
                        for m in range(MT):
                            if t == TP * hf:
                                pe.wait_ge(f_lo, MT * hf + m + 1)
                            for part in (h_hi, h_lo):
                                mm = pe.matmul(ps_dn[t % 2][:], part[:, m, (t % TP) * P:(t % TP + 1) * P], wd_32[:, m, :],
                                               start=(m == 0 and part is h_hi), stop=(m == MT - 1 and part is h_lo))
                        mm.then_inc(f_dn, 1)


def kernel(**inputs):
    import numpy as np
    import concourse.bacc as bacc
    from concourse.bass_utils import run_bass_kernel_spmd

    a = {n.removeprefix("L0_attn_").removeprefix("L0_ffn_"): np.asarray(v) for n, v in inputs.items()}

    def halves(w):
        return w.reshape(w.shape[0], -1, P // 2, 2).swapaxes(2, 3).reshape(w.shape)

    q_c = halves(a["q_codes"]).reshape(KT, P, NKV, HPG, P).transpose(2, 1, 3, 0, 4)
    q_s = halves(a["q_scales"]).reshape(KT, NKV, HPG, P).transpose(1, 2, 0, 3)
    k_c = halves(a["k_codes"]).reshape(KT, P, NKV, P).transpose(2, 1, 0, 3)
    k_s = halves(a["k_scales"]).reshape(KT, NKV, P).transpose(1, 0, 2)
    e_s = np.concatenate([k_s[:, None], q_s], 1)[:, :, 0:EX].transpose(0, 3, 1, 2).reshape(NKV, P, -1)
    q_s, k_s = q_s[:, :, EX:].reshape(NKV, HPG, -1), k_s[:, EX:].reshape(NKV, -1)
    v_c = a["v_codes"].reshape(KT, P, 2, HALF).transpose(2, 1, 0, 3).reshape(2, P, -1)
    v_s = a["v_scales"].reshape(KT, 2, HALF).transpose(1, 0, 2).reshape(2, -1)
    o_c = a["o_codes"].reshape(NKV, HPG, P, HID).transpose(0, 2, 1, 3)
    o_s = a["o_scales"].reshape(NKV, -1)

    def ffn(w):
        return w.reshape(2, MH, P, KT, P).transpose(0, 4, 1, 3, 2).reshape(2, P, -1)

    w_d = a["W_down"].reshape(HID, MT, P).transpose(2, 1, 0)

    inv_freq = (1.0 / np.float32(10000.0) ** (np.arange(0, P, 2, dtype=np.float32) / np.float32(P))).astype(np.float32)
    angle = inv_freq[:, None] * np.arange(SEQ, dtype=np.float32)[None, :]
    cos = np.concatenate([np.cos(angle)] * 2).astype(np.float32)
    sin = np.concatenate([-np.sin(angle), np.sin(angle)]).astype(np.float32)
    mask = np.zeros((P, SEQ), np.float32)
    mask[:, P:] = np.where(np.arange(P)[None, :] <= np.arange(P)[:, None], 0.0, MASKED)

    arrays = {
        "x": a["hidden_states"].reshape(TT, P, HID), "qc": q_c, "qs": q_s, "kc": k_c, "ks": k_s, "es": e_s, "vc": v_c, "vs": v_s,
        "oc": o_c, "os": o_s, "wg": ffn(a["W_gate"]), "wu": ffn(a["W_up"]), "wd": w_d,
        "rope_cos": cos, "rope_sin": sin, "causal": mask, "eye": np.eye(P, dtype=np.float32),
    }
    arrays = {n: np.ascontiguousarray(v) for n, v in arrays.items()}
    nc = bacc.Bacc("TRN2", target_bir_lowering=False, num_devices=1)
    args = [nc.dram_tensor(n, v.shape, mybir.dt.from_np(v.dtype), kind="ExternalInput").ap() for n, v in arrays.items()]
    y = nc.dram_tensor("y", (TT, P, HID), F32, kind="ExternalOutput").ap()
    layer_kernel(nc, *args, y)
    r = run_bass_kernel_spmd(nc, [arrays], core_ids=[0])
    return r.results[0]["y"].reshape(BATCH, SEQ, HID)
```
